# Optimizing a Trainium2 kernel written in Bass

```python
import numpy as np
import jax
import jax.numpy as jnp

def _softmax(x, axis=-1):
    return jax.nn.softmax(x, axis=axis)

def _gelu(x):
    return jax.nn.gelu(x, approximate=True)

def _silu(x):
    return jax.nn.silu(x)

def _sigmoid(x):
    return jax.nn.sigmoid(x)

def _layernorm(x, axis=-1, eps=1e-05):
    m = jnp.mean(x, axis=axis, keepdims=True)
    v = jnp.var(x, axis=axis, keepdims=True)
    return (x - m) / jnp.sqrt(v + eps)

def _scatter_add(tgt, idx, src, axis=0):
    return tgt.at[idx].add(src)

def _segment_sum(src, seg, n):
    return jax.ops.segment_sum(src, seg, n)
kernel_name = 'mk_macaron_d1_jaxref_r8_9af003'

def setup_inputs(seed: int=0):
    np.random.seed(seed)
    _w = jnp.asarray

    def _L0_attn_setup():
        import jax, jax.numpy as jnp
        import numpy as np
        D_MODEL, N_QUERY, N_HEAD = (128, 2, 8)
        D_HEAD = D_MODEL // (N_QUERY * N_HEAD)
        KV = D_HEAD * N_HEAD

        def _reference_tuple_inner(x, Wq, Wk, Wv, memory, memory_norm, memory_weight):
            B, S, _ = x.shape
            QH = N_QUERY * N_HEAD
            scale = 1.0 / jnp.sqrt(jnp.float32(D_HEAD))
            q = x @ Wq
            k = x @ Wk
            v = x @ Wv
            q4 = q.reshape(B, S, QH, D_HEAD)
            k4 = jnp.repeat(k.reshape(B, S, N_HEAD, D_HEAD), N_QUERY, axis=2)
            v4 = jnp.repeat(v.reshape(B, S, N_HEAD, D_HEAD), N_QUERY, axis=2)
            scores = jnp.einsum('bsnd,btnd->bnst', q4, k4) * scale
            probs = jax.nn.softmax(scores, axis=-1)
            a_dot = jnp.einsum('bnst,btnd->bsnd', probs, v4)
            sigma_q = jax.nn.elu(q.reshape(B, S, N_QUERY, KV))
            num = sigma_q @ memory
            den = (sigma_q @ memory_norm)[..., None]
            a_mem = (num / den).reshape(B, S, QH, D_HEAD)
            sigma_k = jax.nn.elu(k)
            retrieved = sigma_k @ memory / (sigma_k @ memory_norm)[..., None]
            new_memory = memory + jnp.einsum('bsk,bsv->kv', sigma_k, v - retrieved)
            new_memory_norm = memory_norm + jnp.sum(sigma_k, axis=(0, 1))
            w = jax.nn.sigmoid(memory_weight)
            out = (a_dot * (1.0 - w) + a_mem * w).reshape(B, S, D_MODEL)
            return (out, new_memory, new_memory_norm)
        key = jax.random.key(seed)
        ks = jax.random.split(key, 6)
        B, S = (2, 256)
        x = jax.random.normal(ks[0], (B, S, D_MODEL), jnp.float32)
        Wq = jax.random.normal(ks[1], (D_MODEL, D_MODEL), jnp.float32) / np.sqrt(D_MODEL)
        Wk = jax.random.normal(ks[2], (D_MODEL, KV), jnp.float32) / np.sqrt(D_MODEL)
        Wv = jax.random.normal(ks[3], (D_MODEL, KV), jnp.float32) / np.sqrt(D_MODEL)
        memory = jax.random.normal(ks[4], (KV, KV), jnp.float32)
        memory_norm = jnp.ones((KV,), jnp.float32)
        memory_weight = jnp.ones((1,), jnp.float32)
        return {'x': x, 'Wq': Wq, 'Wk': Wk, 'Wv': Wv, 'memory': memory, 'memory_norm': memory_norm, 'memory_weight': memory_weight}
    _L0_attn_in = _L0_attn_setup()

    def _L0_ffn_setup():
        import jax, jax.numpy as jnp
        import numpy as np
        DIM = 128
        HIDDEN = 384
        SCALE = 1.0 / 127.0

        def _dequant(w_int, dtype):
            return w_int.astype(dtype) * jnp.asarray(SCALE, dtype)
        key = jax.random.key(seed)
        k_x, k_g, k_u, k_d = jax.random.split(key, 4)
        x = jax.random.normal(k_x, (4, 256, DIM), dtype=jnp.float32)
        w_gate = jax.random.randint(k_g, (HIDDEN, DIM), -127, 128, dtype=jnp.int32)
        w_up = jax.random.randint(k_u, (HIDDEN, DIM), -127, 128, dtype=jnp.int32)
        w_down = jax.random.randint(k_d, (DIM, HIDDEN), -127, 128, dtype=jnp.int32)
        return {'x': x, 'w_gate': w_gate, 'w_up': w_up, 'w_down': w_down}
    _L0_ffn_in = _L0_ffn_setup()
    _d = {'L0_attn_x': _L0_attn_in['x'], 'L0_attn_Wq': _L0_attn_in['Wq'], 'L0_attn_Wk': _L0_attn_in['Wk'], 'L0_attn_Wv': _L0_attn_in['Wv'], 'L0_attn_memory': _L0_attn_in['memory'], 'L0_attn_memory_norm': _L0_attn_in['memory_norm'], 'L0_attn_memory_weight': _L0_attn_in['memory_weight'], 'L0_ffn_w_gate': _L0_ffn_in['w_gate'], 'L0_ffn_w_up': _L0_ffn_in['w_up'], 'L0_ffn_w_down': _L0_ffn_in['w_down']}
    _x0 = _d['L0_attn_x']
    _d['L0_attn_x'] = jax.random.normal(jax.random.fold_in(jax.random.key(seed), 1), (4, 1024, 128), dtype=_x0.dtype)
    del _x0
    return _d

def reference(L0_attn_x, L0_attn_Wq, L0_attn_Wk, L0_attn_Wv, L0_attn_memory, L0_attn_memory_norm, L0_attn_memory_weight, L0_ffn_w_gate, L0_ffn_w_up, L0_ffn_w_down):

    def _L0_attn_ref(x, Wq, Wk, Wv, memory, memory_norm, memory_weight):
        import jax, jax.numpy as jnp
        import numpy as np
        D_MODEL, N_QUERY, N_HEAD = (128, 2, 8)
        D_HEAD = D_MODEL // (N_QUERY * N_HEAD)
        KV = D_HEAD * N_HEAD

        def _reference_tuple_inner(x, Wq, Wk, Wv, memory, memory_norm, memory_weight):
            B, S, _ = x.shape
            QH = N_QUERY * N_HEAD
            scale = 1.0 / jnp.sqrt(jnp.float32(D_HEAD))
            q = x @ Wq
            k = x @ Wk
            v = x @ Wv
            q4 = q.reshape(B, S, QH, D_HEAD)
            k4 = jnp.repeat(k.reshape(B, S, N_HEAD, D_HEAD), N_QUERY, axis=2)
            v4 = jnp.repeat(v.reshape(B, S, N_HEAD, D_HEAD), N_QUERY, axis=2)
            scores = jnp.einsum('bsnd,btnd->bnst', q4, k4) * scale
            probs = jax.nn.softmax(scores, axis=-1)
            a_dot = jnp.einsum('bnst,btnd->bsnd', probs, v4)
            sigma_q = jax.nn.elu(q.reshape(B, S, N_QUERY, KV))
            num = sigma_q @ memory
            den = (sigma_q @ memory_norm)[..., None]
            a_mem = (num / den).reshape(B, S, QH, D_HEAD)
            sigma_k = jax.nn.elu(k)
            retrieved = sigma_k @ memory / (sigma_k @ memory_norm)[..., None]
            new_memory = memory + jnp.einsum('bsk,bsv->kv', sigma_k, v - retrieved)
            new_memory_norm = memory_norm + jnp.sum(sigma_k, axis=(0, 1))
            w = jax.nn.sigmoid(memory_weight)
            out = (a_dot * (1.0 - w) + a_mem * w).reshape(B, S, D_MODEL)
            return (out, new_memory, new_memory_norm)
        return _reference_tuple_inner(x, Wq, Wk, Wv, memory, memory_norm, memory_weight)[0]

    def _L0_ffn_ref(x, w_gate, w_up, w_down):
        import jax, jax.numpy as jnp
        import numpy as np
        DIM = 128
        HIDDEN = 384
        SCALE = 1.0 / 127.0

        def _dequant(w_int, dtype):
            return w_int.astype(dtype) * jnp.asarray(SCALE, dtype)
        wg = _dequant(w_gate, x.dtype)
        wu = _dequant(w_up, x.dtype)
        wd = _dequant(w_down, x.dtype)
        gate = jnp.einsum('bsd,hd->bsh', x, wg)
        up = jnp.einsum('bsd,hd->bsh', x, wu)
        h = jax.nn.silu(gate) * up
        return jnp.einsum('bsh,dh->bsd', h, wd)
    x = L0_attn_x
    x = x + 0.5 * _L0_ffn_ref(_layernorm(x, axis=-1), L0_ffn_w_gate, L0_ffn_w_up, L0_ffn_w_down)
    x = x + _L0_attn_ref(_layernorm(x, axis=-1), L0_attn_Wq, L0_attn_Wk, L0_attn_Wv, L0_attn_memory, L0_attn_memory_norm, L0_attn_memory_weight)
    x = x + 0.5 * _L0_ffn_ref(_layernorm(x, axis=-1), L0_ffn_w_gate, L0_ffn_w_up, L0_ffn_w_down)
    return x

_drawn_inputs = setup_inputs


def setup_inputs(seed=0):
    import zlib

    import numpy as np

    out = dict(_drawn_inputs(seed))
    spreads = {'L0_attn_memory_norm': (1.0, 0.2)}
    factors = {'L0_attn_Wk': 38.181, 'L0_attn_Wv': 37.703}
    for name, (base, spread) in spreads.items():
        noise = np.random.default_rng([zlib.crc32(name.encode()), seed]).standard_normal(out[name].shape)
        drawn = base * np.exp(spread * noise) if base else spread * noise
        out[name] = jnp.asarray(drawn.astype(out[name].dtype))
    for name, factor in factors.items():
        out[name] = (out[name] * factor).astype(out[name].dtype)
    return out
```

```python
from contextlib import ExitStack

import concourse.bass as bass
from concourse import mybir

P = 128
B, S, D = 4, 1024, 128
HEADS_KV, GROUP, DH = 8, 2, 8
KV = HEADS_KV * DH
HID = 384
KH = HID // P
CH = 512
TPC = CH // P
CHUNKS = B * S // CH
TILES = S // P
PAIRS = B * HEADS_KV
PARTS = 3
QROWS = PARTS * PARTS * DH
MAXROW = 96
SLOTS = 4
LEAD = 3
LN_EPS = 1e-5
FFN_SCALE = 1.0 / 127.0
TANH_SCALE = 0.5 * FFN_SCALE
Y_SCALE = 0.5 * 0.5 * FFN_SCALE ** 3
SM_SCALE = float(DH) ** -0.5
VW = DH + 1
VPAD = 32
MCOLS = GROUP * PARTS * TILES


def build(nc, x, wq, wk, wv, memory, memory_norm, memory_weight, wg_t, wu_t, wd_t, out):
    f32, bf16, i32 = mybir.dt.float32, mybir.dt.bfloat16, mybir.dt.int32
    ALU, ACT, AX = mybir.AluOpType, mybir.ActivationFunctionType, mybir.AxisListType

    q_spill = nc.dram_tensor("q_spill", [PAIRS, PARTS, GROUP * DH, S], bf16, kind="Internal").ap()
    k_spill = nc.dram_tensor("k_spill", [PAIRS, PARTS, DH, S], bf16, kind="Internal").ap()
    x_rows = x.rearrange("b (t p) d -> p (b t) d", p=P)
    out_rows = out.rearrange("b (t p) d -> p (b t) d", p=P)

    ctx = ExitStack()
    with ctx:
        def sb(name, shape, dt=f32):
            return ctx.enter_context(nc.sbuf_tensor(name, shape, dt))

        def bank(name):
            return ctx.enter_context(nc.psum_tensor(name, [P, 512], f32))

        def sem(name):
            return ctx.enter_context(nc.semaphore(name))

        ident = sb("ident", [P, P])
        ident_b = sb("ident_b", [P, P], bf16)
        wq_s, wk_s, wv_s = sb("wq_s", [P, D]), sb("wk_s", [P, KV]), sb("wv_s", [P, KV])
        mem_s = sb("mem_s", [P, D])
        norm_s = sb("norm_s", [P, GROUP])
        w_int = sb("w_int", [P, 3, HID], i32)
        w_f = sb("w_f", [P, 3, HID])
        mw = sb("mw", [P, 1])
        mix = sb("mix", [P, 6])
        w_col, omw_col = mix[:, 4:5], mix[:, 5:6]
        x_c = sb("x_c", [P, 2, TPC, D])
        st6 = sb("st6", [P, TPC, 6])
        mv = sb("mv", [P, 2, TPC, 2])
        rstd = sb("rstd", [P, 2, TPC])
        neg_half = sb("neg_half", [P, TPC])
        x_hat = sb("x_hat", [P, 2, TPC, D])
        x_t = sb("x_t", [P, 2, CH])
        th = sb("th", [P, 2, CH])
        gated = sb("gated", [P, 2, CH])
        hid = sb("hid", [P, 2, KH, CH])
        out_c = sb("out_c", [P, 2, TPC, D])
        x1_c = sb("x1_c", [P, 2, TPC, D])
        st6b = sb("st6b", [P, TPC, 6])
        mvb = sb("mvb", [P, TPC, 2])
        rstdb = sb("rstdb", [P, 2, TPC])
        xn_hat = sb("xn_hat", [P, TPC, D])
        xn_t = sb("xn_t", [P, CH])
        q_p = sb("q_p", [P, 2, PARTS, CH], bf16)
        k_p = sb("k_p", [KV, 2, PARTS, CH], bf16)
        q_r, k_r = sb("q_r", [P, CH]), sb("k_r", [KV, CH])
        q_neg, q_exp, q_elu = sb("q_neg", [P, CH]), sb("q_exp", [P, CH]), sb("q_elu", [P, CH])
        r_den = sb("r_den", [P, 2, TPC * GROUP])
        a_mem = sb("a_mem", [P, TPC, D])
        v_all = sb("v_all", [P, PAIRS, TILES * VW])
        xm = sb("xm", [P, PAIRS, TILES, GROUP * DH])
        q_op = sb("q_op", [P, SLOTS, GROUP, S], bf16)
        k_op = sb("k_op", [P, SLOTS, S], bf16)
        mx = sb("mx", [P, 2, GROUP, TILES, 2])
        m16 = sb("m16", [P, 2, GROUP, TILES])
        m_neg, m_res = sb("m_neg", [P, GROUP, TILES]), sb("m_res", [P, GROUP, TILES])
        m_parts = sb("m_parts", [P, 2, GROUP, PARTS, TILES], bf16)
        m_rows = sb("m_rows", [MCOLS, 2, P], bf16)
        probs = sb("probs", [P, 2, 2 * GROUP, 512])
        v9 = sb("v9", [P, 2, TILES, VPAD])
        o_t = sb("o_t", [P, 2, 512])
        r_sum = sb("r_sum", [P, 2, 4, 4])
        o_n = sb("o_n", [P, 2, 4, GROUP, DH])

        banks = [bank(f"bank{n}") for n in range(8)]
        gate_b, up_b = (banks[0], banks[2]), (banks[1], banks[3])
        tr_b, y_b, q_b, k_b = banks[4], banks[5], banks[6], banks[7]
        a_b, t_b, pv_b, misc_b = banks[0:3], banks[3:6], banks[6], banks[7]

        x_in, w_loaded = [sem("x_in0"), sem("x_in1")], sem("w_loaded")
        mem_loaded, mw_loaded = sem("mem_loaded"), sem("mw_loaded")
        zeroed, ones_set, ident_set, op_set = sem("zeroed"), sem("ones_set"), sem("ident_set"), sem("op_set")
        w_cast, mw_exp, mix_step = sem("w_cast"), sem("mw_exp"), sem("mix_step")

        class FfnSems:
            def __init__(self, tag):
                self.src, self.ln, self.root, self.xhat = (sem(f"{tag}_{n}") for n in ("src", "ln", "root", "xhat"))
                self.xt_ps, self.xt, self.gu, self.th = (sem(f"{tag}_{n}") for n in ("xt_ps", "xt", "gu", "th"))
                self.gated, self.hidden, self.y, self.res = (
                    sem(f"{tag}_{n}") for n in ("gated", "hidden", "y", "res"))

        f1, f3 = FfnSems("ffn1"), FfnSems("ffn2")
        ln2, root2, xn_ready, xn_ps, xn_sb = sem("ln2"), sem("root2"), sem("xn_ready"), sem("xn_ps"), sem("xn_sb")
        q_ps, k_ps, v_ps, v_sb = sem("q_ps"), sem("k_ps"), sem("v_ps"), sem("v_sb")
        q1_done, q_res, q2_done, q3_done = sem("q1_done"), sem("q_res"), sem("q2_done"), sem("q3_done")
        k1_done, k_res, k2_done, k3_done = sem("k1_done"), sem("k_res"), sem("k2_done"), sem("k3_done")
        q_min, q_expd, q_elud, am_ps = sem("q_min"), sem("q_expd"), sem("q_elud"), sem("am_ps")
        am_step, am_done, xm_done = sem("am_step"), sem("am_done"), sem("xm_done")
        spilled = [sem("spilled0"), sem("spilled1")]
        loaded = [sem(f"loaded{s}") for s in range(SLOTS)]
        a_ready, a_used, m_max, m_split, m_ps, m_sb, m_in = (
            sem(n) for n in ("a_ready", "a_used", "m_max", "m_split", "m_ps", "m_sb", "m_in"))
        t_ready, p_ready, pv_done, pv_sb = (sem(n) for n in ("t_ready", "p_ready", "pv_done", "pv_sb"))
        v9_ready, o_ps, o_step, o_norm, xm_added = (
            sem(n) for n in ("v9_ready", "o_ps", "o_step", "o_norm", "xm_added"))
        stored = [sem("stored0"), sem("stored1")]
        waits_passed = sem("waits_passed")
        LOADS = 2 * PARTS + 1
        block = ctx.enter_context(nc.Block())

        def at(n, c, k):
            return c * n + k

        def chunk_loop(eng, body, first=0):
            body(0, True)
            with eng.Fori(1, CHUNKS // 2) as pair:
                body(pair, False)

        def attention_loop(eng, body):
            body(0, True, False)
            with eng.Fori(1, PAIRS // SLOTS - 1) as it:
                body(it, False, False)
            body(PAIRS // SLOTS - 1, False, True)

        def wait_alone(eng, semaphore, count):
            eng.wait_ge(semaphore, count)
            if not isinstance(count, int):
                eng.sem_inc(waits_passed, 1)

        def ahead(i):
            return (1, i + LEAD) if i + LEAD < TILES else (2, i + LEAD - TILES)

        @block.sync
        def _(sp):
            def load_x(pair, h):
                if not isinstance(pair, int) or pair > 0:
                    sp.wait_ge(f1.res, at(2, pair, h - 1))
                sp.dma_start(x_c[:, h, :, :], x_rows[:, bass.ds(pair * (2 * TPC) + h * TPC, TPC), :]
                             ).then_inc(x_in[h], 16)

            load_x(0, 0)
            load_x(0, 1)
            for n, w in enumerate((wg_t, wu_t)):
                sp.dma_start(w_int[:, n, :], w).then_inc(w_loaded, 16)
            sp.dma_start(w_int[:, 2, :].rearrange("p (k d) -> p k d", k=KH),
                         wd_t.rearrange("(k p) d -> p k d", p=P)).then_inc(w_loaded, 16)
            sp.dma_start(wq_s[:, :], wq).then_inc(mem_loaded, 16)
            sp.dma_start(wk_s[:, :], wk).then_inc(mem_loaded, 16)
            sp.dma_start(wv_s[:, :], wv).then_inc(mem_loaded, 16)
            sp.wait_ge(zeroed, 1)
            for g in range(GROUP):
                sp.dma_start(mem_s[KV * g:KV * g + KV, KV * g:KV * g + KV], memory).then_inc(mem_loaded, 16)
                sp.dma_start(norm_s[KV * g:KV * g + KV, g:g + 1],
                             memory_norm.rearrange("(n a) -> n a", a=1)).then_inc(mem_loaded, 16)

            def load_pair(J, slot):
                for g in range(GROUP):
                    for a in range(PARTS):
                        sp.dma_start(q_op[PARTS * DH * a:PARTS * DH * (a + 1), slot, g, :],
                                     repeated_part(J, a, g)).then_inc(loaded[slot], 16)
                sp.dma_start(k_op[0:QROWS, slot, :], repeated_keys(J)).then_inc(loaded[slot], 16)

            def repeated_part(J, a, g):
                v = q_spill[J, a, DH * g:DH * g + DH, :]
                return bass.AP(v.tensor, v.offset, [[0, PARTS], [S, DH], [1, S]])

            def repeated_keys(J):
                v = k_spill[J, 0, 0, :]
                return bass.AP(v.tensor, v.offset, [[0, PARTS], [S, PARTS * DH], [1, S]])

            def spill(pair, h):
                sp.wait_ge(q3_done, at(2, pair, h + 1))
                for j in range(HEADS_KV):
                    R = GROUP * DH
                    dst = q_spill[pair * HEADS_KV + j, :, :, h * CH:(h + 1) * CH]
                    sp.dma_start(dst.rearrange("a r s -> r a s"),
                                 q_p[R * j:R * j + R, h, :, :]).then_inc(spilled[h], 16)
                sp.wait_ge(k3_done, at(2, pair, h + 1))
                for j in range(HEADS_KV):
                    dst = k_spill[pair * HEADS_KV + j, :, :, h * CH:(h + 1) * CH]
                    sp.dma_start(dst.rearrange("a r s -> r a s"),
                                 k_p[DH * j:DH * j + DH, h, :, :]).then_inc(spilled[h], 16)
            SP = 2 * HEADS_KV * 16

            load_x(1, 0)
            spill(0, 0)
            with sp.Fori(1, CHUNKS // 2 - 1) as pair:
                load_x(pair, 1)
                spill(pair - 1, 1)
                load_x(pair + 1, 0)
                spill(pair, 0)
            load_x(CHUNKS // 2 - 1, 1)
            spill(CHUNKS // 2 - 2, 1)
            spill(CHUNKS // 2 - 1, 0)
            sp.wait_ge(op_set, 2)
            sp.wait_ge(spilled[0], SP)
            sp.wait_ge(spilled[1], SP)
            for s in range(SLOTS - 1):
                load_pair(s, s)
            spill(CHUNKS // 2 - 1, 1)

            def m_to_operand(K, slot, par):
                sp.wait_ge(m_sb, at(1, K, 1))
                half = PARTS * TILES
                for g in range(GROUP):
                    for a in range(PARTS):
                        sp.dma_start(q_op[MAXROW + a:MAXROW + a + 1, slot, g, :].rearrange("a (t p) -> a t p", p=P),
                                     m_rows[half * g + TILES * a:half * g + TILES * (a + 1), par, :]
                                     ).then_inc(m_in, 16)

            m_to_operand(0, 0, 0)
            for h in range(2):
                sp.wait_ge(spilled[h], SP * (CHUNKS // 2))

            def pairs(it, first, last):
                for u in range(SLOTS):
                    J = it * SLOTS + u
                    if not (last and u > 0):
                        if not (first and u == 0):
                            sp.wait_ge(t_ready, at(32, J, 0))
                        load_pair(J + SLOTS - 1, (u + SLOTS - 1) % SLOTS)
                    if not (last and u == SLOTS - 1):
                        m_to_operand(J + 1, (u + 1) % SLOTS, (u + 1) % 2)

            attention_loop(sp, pairs)

            def store(pair, h):
                sp.wait_ge(f3.res, at(2, pair, h + 1))
                sp.dma_start(out_rows[:, bass.ds(pair * (2 * TPC) + h * TPC, TPC), :],
                             out_c[:, h, :, :]).then_inc(stored[h], 16)

            with sp.Fori(0, CHUNKS // 2) as pair:
                store(pair, 0)
                store(pair, 1)
            for h in range(2):
                sp.wait_ge(stored[h], 16 * (CHUNKS // 2))

        @block.gpsimd
        def _(pool):
            pool.memset(neg_half[:, :], -0.5)
            pool.memset(mem_s[:, :], 0.0)
            pool.memset(norm_s[:, :], 0.0).then_inc(zeroed, 1)
            pool.memset(ident[:, :], 0.0)
            pool.memset(ident_b[:, :], 0.0).then_inc(ident_set, 1)
            pool.wait_ge(ident_set, 1)
            for m in (ident, ident_b):
                pool.affine_select(out=m[:, :], in_=m[:, :], compare_op=ALU.not_equal, fill=1.0, base=0,
                                   pattern=[[-1, P]], channel_multiplier=1).then_inc(ident_set, 1)

            def x1_plus_memory(pair, h):
                wait_alone(pool, am_done, at(2, pair, h + 1))
                dst = xm[:, bass.ds(pair * HEADS_KV, HEADS_KV), h * TPC:(h + 1) * TPC, :]
                for m in range(TPC):
                    i = pool.tensor_tensor(
                        dst[:, :, m, :], a_mem[:, m, :].rearrange("p (j e) -> p j e", j=HEADS_KV),
                        x1_c[:, h, m, :].rearrange("p (j e) -> p j e", j=HEADS_KV), ALU.add)
                i.then_inc(xm_done, 1)

            def normalise(src, dst, agg, rs, steps, n, ready):
                pool.tensor_scalar(rs[:, 0, :], agg[:, :, 1], LN_EPS, None, ALU.add).then_inc(steps, 1)
                wait_alone(pool, steps, n + 1)
                pool.tensor_tensor(rs[:, 1, :], rs[:, 0, :], neg_half[:, :], ALU.pow).then_inc(steps, 1)
                wait_alone(pool, steps, n + 2)
                for m in range(TPC):
                    i = pool.tensor_scalar(dst(m), src(m), agg[:, m, 0:1], rs[:, 1, m:m + 1],
                                           ALU.subtract, ALU.mult)
                i.then_inc(ready, 1)

            def ffn_norm(f, pair, h):
                wait_alone(pool, f.ln, at(4, pair, 2 * h + 2))
                if not isinstance(pair, int) or pair > 0:
                    wait_alone(pool, f.xt_ps, at(2, pair, h - 1))
                normalise(lambda m: x_c[:, h, m, :], lambda m: x_hat[:, h, m, :], mv[:, h, :, :],
                          rstd, f.root, at(4, pair, 2 * h), f.xhat)

            def proj_norm(pair, h):
                wait_alone(pool, ln2, at(4, pair, 2 * h + 2))
                if not (isinstance(pair, int) and pair == 0 and h == 0):
                    wait_alone(pool, xn_ps, at(2, pair, h))
                normalise(lambda m: x1_c[:, h, m, :], lambda m: xn_hat[:, m, :], mvb, rstdb, root2,
                          at(4, pair, 2 * h), xn_ready)

            ffn_norm(f1, 0, 0)

            def phase1(pair, first, last=False):
                for h in range(2):
                    if h == 0:
                        ffn_norm(f1, pair, 1)
                    elif not last:
                        ffn_norm(f1, pair + 1, 0)
                    proj_norm(pair, h)
                    if not (first and h == 0):
                        x1_plus_memory(*((pair, 0) if h else (pair - 1, 1)))

            pool.memset(v_all[:, :, :], 1.0).then_inc(ones_set, 1)
            phase1(0, True)
            pool.memset(v9[:, :, :, :], 0.0)
            pool.memset(q_op[:, :, :, :], 0.0)
            pool.memset(k_op[:, :, :], 0.0).then_inc(op_set, 1)
            pool.wait_ge(op_set, 1)
            pool.memset(k_op[MAXROW:P, :, :], 1.0).then_inc(op_set, 1)
            pool.wait_ge(op_set, 2)
            with pool.Fori(1, CHUNKS // 2 - 1) as pair:
                phase1(pair, False)
            phase1(CHUNKS // 2 - 1, False, True)
            x1_plus_memory(CHUNKS // 2 - 1, 1)

            def split_max(K, par):
                wait_alone(pool, m_max, at(1, K, 1))
                pool.tensor_scalar(m_neg[:, :, :], m16[:, par, :, :], -1.0, None, ALU.mult).then_inc(m_split, 1)
                wait_alone(pool, m_split, at(5, K, 1))
                pool.tensor_copy(m_parts[:, par, :, 0, :], m_neg[:, :, :]).then_inc(m_split, 1)
                wait_alone(pool, m_split, at(5, K, 2))
                pool.tensor_tensor(m_res[:, :, :], m_neg[:, :, :], m_parts[:, par, :, 0, :],
                                   ALU.subtract).then_inc(m_split, 1)
                wait_alone(pool, m_split, at(5, K, 3))
                pool.tensor_copy(m_parts[:, par, :, 1, :], m_res[:, :, :]).then_inc(m_split, 1)
                wait_alone(pool, m_split, at(5, K, 4))
                pool.tensor_tensor(m_parts[:, par, :, 2, :], m_res[:, :, :], m_parts[:, par, :, 1, :],
                                   ALU.subtract).then_inc(m_split, 1)

            def values(J, par):
                pool.tensor_copy(v9[:, par, :, 0:VW], v_all[:, J, :].rearrange("p (t e) -> p t e", t=TILES)
                                 if isinstance(J, int) else
                                 v_all[:, bass.ds(J, 1), :].rearrange("p a (t e) -> p (a t) e", t=TILES)
                                 ).then_inc(v9_ready, 1)

            def add_attention(J, par):
                wait_alone(pool, o_norm, at(1, J, 1))
                dst = xm[:, bass.ds(J, 1), :, :].rearrange("p a t e -> p (a t) e")
                pool.tensor_tensor(dst, dst, o_n[:, :, :, :, :].rearrange("p h c g d -> p (h c) (g d)"),
                                   ALU.add).then_inc(xm_added, 1)

            wait_alone(pool, v_sb, CHUNKS)
            values(0, 0)
            split_max(0, 0)

            def pairs(it, first, last):
                for u in range(SLOTS):
                    J = it * SLOTS + u
                    if not (last and u == SLOTS - 1):
                        if not (first and u == 0):
                            wait_alone(pool, pv_done, at(1, J, 0))
                        values(J + 1, (u + 1) % 2)
                    if not (first and u == 0):
                        add_attention(J - 1, (u - 1) % 2)
                    if not (last and u == SLOTS - 1):
                        split_max(J + 1, (u + 1) % 2)

            attention_loop(pool, pairs)
            add_attention(PAIRS - 1, 1)
            wait_alone(pool, xm_added, PAIRS)

            def gather_x2(pair, h):
                if not isinstance(pair, int) or pair > 0:
                    wait_alone(pool, f3.res, at(2, pair, h - 1))
                src = xm[:, bass.ds(pair * HEADS_KV, HEADS_KV), h * TPC:(h + 1) * TPC, :]
                for m in range(TPC):
                    i = pool.tensor_copy(x_c[:, h, m, :].rearrange("p (j e) -> p j e", j=HEADS_KV), src[:, :, m, :])
                i.then_inc(f3.src, 1)

            gather_x2(0, 0)
            gather_x2(0, 1)
            ffn_norm(f3, 0, 0)

            def phase3(pair, last=False):
                ffn_norm(f3, pair, 1)
                if not last:
                    for h in range(2):
                        gather_x2(pair + 1, h)
                        if h == 0:
                            ffn_norm(f3, pair + 1, 0)

            with pool.Fori(0, CHUNKS // 2 - 1) as pair:
                phase3(pair)
            phase3(CHUNKS // 2 - 1, True)

        @block.scalar
        def _(act):
            act.dma_start(mw[:, :], bass.AP(memory_weight.tensor, memory_weight.offset, [[0, P], [1, 1]])
                          ).then_inc(mw_loaded, 16)
            act.wait_ge(w_loaded, 16 * 3)
            act.activation(w_f[:, :, :], w_int[:, :, :], ACT.Copy).then_inc(w_cast, 1)
            act.wait_ge(mw_loaded, 16)
            act.activation(mix[:, 0:1], mw[:, :], ACT.Exp, scale=-1.0)
            act.activation(mix[:, 1:2], mw[:, :], ACT.Exp).then_inc(mw_exp, 1)

            def ffn_xt(f, pair, h):
                act.wait_ge(f.xt_ps, at(2, pair, h + 1))
                act.activation(x_t[:, h, :], tr_b[:, :], ACT.Copy).then_inc(f.xt, 1)

            def ffn_tanh(f, pair, h, k):
                n = KH * h + k
                act.wait_ge(f.gu, at(2 * KH, pair, n + 1))
                if not isinstance(pair, int) or pair > 0 or n >= 2:
                    act.wait_ge(f.hidden, at(2 * KH, pair, n - 1))
                act.activation(th[:, n % 2, :], gate_b[n % 2][:, :], ACT.Tanh, scale=TANH_SCALE).then_inc(f.th, 1)

            def proj_xn(pair, h):
                act.wait_ge(xn_ps, at(2, pair, h + 1))
                act.activation(xn_t[:, :], tr_b[:, :], ACT.Copy).then_inc(xn_sb, 1)

            def proj_first(pair, h):
                if not isinstance(pair, int) or pair > 0:
                    act.wait_ge(spilled[h], at(2 * HEADS_KV * 16, pair, 0))
                act.wait_ge(q_ps, at(2, pair, h + 1))
                act.activation(q_p[:, h, 0, :], q_b[:, :], ACT.Copy).then_inc(q1_done, 1)
                act.wait_ge(k_ps, at(2, pair, h + 1))
                act.activation(k_p[:, h, 0, :], k_b[0:KV, :], ACT.Copy).then_inc(k1_done, 1)
                act.wait_ge(v_ps, at(2, pair, h + 1))
                if isinstance(pair, int) and pair == 0 and h == 0:
                    act.wait_ge(ones_set, 1)
                for m in range(TPC):
                    o = (h * TPC + m) * VW
                    i = act.activation(v_all[:, bass.ds(pair * HEADS_KV, HEADS_KV), o:o + DH],
                                       tr_b[:, KV * m:KV * m + KV].rearrange("p (j d) -> p j d", d=DH), ACT.Copy)
                i.then_inc(v_sb, 1)

            def proj_second(pair, h):
                act.wait_ge(q_min, at(2, pair, h + 1))
                act.activation(q_exp[:, :], q_neg[:, :], ACT.Exp).then_inc(q_expd, 1)
                act.wait_ge(q_res, at(2, pair, h + 1))
                act.activation(q_p[:, h, 1, :], q_r[:, :], ACT.Copy).then_inc(q2_done, 1)
                act.wait_ge(k_res, at(2, pair, h + 1))
                act.activation(k_p[:, h, 1, :], k_r[:, :], ACT.Copy).then_inc(k2_done, 1)

            def phase1(pair, first):
                for h in range(2):
                    prev = (pair, 0) if h else (pair - 1, 1)
                    has_prev = not (first and h == 0)
                    ffn_xt(f1, pair, h)
                    ffn_tanh(f1, pair, h, 0)
                    if has_prev:
                        proj_xn(*prev)
                    ffn_tanh(f1, pair, h, 1)
                    if has_prev:
                        proj_first(*prev)
                    ffn_tanh(f1, pair, h, 2)
                    if has_prev:
                        proj_second(*prev)

            chunk_loop(act, phase1)
            proj_xn(CHUNKS // 2 - 1, 1)
            proj_first(CHUNKS // 2 - 1, 1)
            proj_second(CHUNKS // 2 - 1, 1)

            def max_rows(K, par):
                act.wait_ge(m_ps, at(1, K, 1))
                act.activation(m_rows[:, par, :], misc_b[:, :].bitcast(bf16)[0:MCOLS, 0:P], ACT.Copy
                               ).then_inc(m_sb, 1)

            def pv_out(J, par):
                act.wait_ge(pv_done, at(1, J, 1))
                act.activation(o_t[:, par, :], pv_b[:, :], ACT.Copy).then_inc(pv_sb, 1)

            max_rows(0, 0)

            def pairs(it, first, last):
                for u in range(SLOTS):
                    J = it * SLOTS + u
                    for i in range(TILES):
                        for q in range(2 * GROUP):
                            act.wait_ge(t_ready, at(32, J, 4 * i + q + 1))
                            act.activation(probs[:, i % 2, q, :], t_b[(4 * i + q) % 3][:, :], ACT.Exp,
                                           scale=SM_SCALE).then_inc(p_ready, 1)
                            if i == 6 and q == 1 and not (last and u == SLOTS - 1):
                                max_rows(J + 1, (u + 1) % 2)
                        if i == 0 and not (first and u == 0):
                            pv_out(J - 1, (u - 1) % 2)

            attention_loop(act, pairs)
            pv_out(PAIRS - 1, 1)

            def phase3(pair):
                for h in range(2):
                    ffn_xt(f3, pair, h)
                    for k in range(KH):
                        ffn_tanh(f3, pair, h, k)

            phase3(0)
            with act.Fori(1, CHUNKS // 2) as pair:
                phase3(pair)

        @block.vector
        def _(dve):
            def moments(src, s6, agg, steps, n):
                for m in range(TPC):
                    i = dve.bn_stats(s6[:, m, :], src(m))
                i.then_inc(steps, 1)
                wait_alone(dve, steps, n + 1)
                for m in range(TPC):
                    i = dve.bn_aggr(agg[:, m, :], s6[:, m, :])
                i.then_inc(steps, 1)

            def ffn_moments(f, pair, h):
                if not isinstance(pair, int) or pair > 0:
                    dve.wait_ge(f.xhat, at(2, pair, h - 1))
                if f is f1:
                    dve.wait_ge(x_in[h], at(16, pair, 16))
                else:
                    dve.wait_ge(f.src, at(2, pair, h + 1))
                moments(lambda m: x_c[:, h, m, :], st6, mv[:, h, :, :], f.ln, at(4, pair, 2 * h))

            def ffn_hidden(f, pair, h, k):
                n = KH * h + k
                dve.wait_ge(f.th, at(2 * KH, pair, n + 1))
                dve.scalar_tensor_tensor(gated[:, n % 2, :], th[:, n % 2, :], 1.0, gate_b[n % 2][:, :],
                                         ALU.add, ALU.mult).then_inc(f.gated, 1)
                dve.wait_ge(f.gated, at(2 * KH, pair, n + 1))
                dve.tensor_tensor(hid[:, h, k, :], gated[:, n % 2, :], up_b[n % 2][:, :],
                                  ALU.mult).then_inc(f.hidden, 1)

            def ffn_residual(f, pair, h):
                dve.wait_ge(f.y, at(2, pair, h + 1))
                if f is f1:
                    if not isinstance(pair, int) or pair > 0:
                        dve.wait_ge(xm_done, at(2, pair, h - 1))
                    dst = x1_c[:, h, :, :]
                else:
                    if not isinstance(pair, int) or pair > 0:
                        dve.wait_ge(stored[h], at(16, pair, 0))
                    dst = out_c[:, h, :, :]
                dve.scalar_tensor_tensor(dst.rearrange("p t d -> p (t d)"), y_b[:, :], Y_SCALE,
                                         x_c[:, h, :, :].rearrange("p t d -> p (t d)"), ALU.mult, ALU.add).then_inc(f.res, 1)

            def proj_moments(pair, h):
                dve.wait_ge(f1.res, at(2, pair, h + 1))
                if not (isinstance(pair, int) and pair == 0 and h == 0):
                    dve.wait_ge(xn_ready, at(2, pair, h))
                moments(lambda m: x1_c[:, h, m, :], st6b, mvb[:, :, :], ln2, at(4, pair, 2 * h))

            def proj_residues(pair, h):
                dve.wait_ge(q1_done, at(2, pair, h + 1))
                dve.tensor_scalar(q_neg[:, :], q_b[:, :], 0.0, None, ALU.min).then_inc(q_min, 1)
                dve.tensor_tensor(q_r[:, :], q_b[:, :], q_p[:, h, 0, :], ALU.subtract).then_inc(q_res, 1)
                dve.wait_ge(k1_done, at(2, pair, h + 1))
                dve.tensor_tensor(k_r[:, :], k_b[0:KV, :], k_p[:, h, 0, :], ALU.subtract).then_inc(k_res, 1)

            def proj_thirds(pair, h):
                dve.wait_ge(q_expd, at(2, pair, h + 1))
                dve.scalar_tensor_tensor(q_elu[:, :], q_exp[:, :], -1.0, q_b[:, :], ALU.add, ALU.max
                                         ).then_inc(q_elud, 1)
                dve.wait_ge(q2_done, at(2, pair, h + 1))
                dve.tensor_tensor(q_p[:, h, 2, :], q_r[:, :], q_p[:, h, 1, :], ALU.subtract).then_inc(q3_done, 1)
                dve.wait_ge(k2_done, at(2, pair, h + 1))
                dve.tensor_tensor(k_p[:, h, 2, :], k_r[:, :], k_p[:, h, 1, :], ALU.subtract).then_inc(k3_done, 1)

            def memory_read(pair, h):
                dve.wait_ge(am_ps, at(2, pair, h + 1))
                dve.reciprocal(r_den[:, 0, :], k_b[:, 0:TPC * GROUP]).then_inc(am_step, 1)
                dve.wait_ge(am_step, at(4, pair, 2 * h + 1))
                dve.tensor_scalar(r_den[:, 1, :], r_den[:, 0, :], w_col, None, ALU.mult).then_inc(am_step, 1)
                dve.wait_ge(am_step, at(4, pair, 2 * h + 2))
                if not (isinstance(pair, int) and pair == 0 and h == 0):
                    dve.wait_ge(xm_done, at(2, pair, h))
                dve.tensor_tensor(a_mem[:, :, :].rearrange("p t (g e) -> p (t g) e", g=GROUP),
                                  q_b[:, :].rearrange("p (n e) -> p n e", e=KV),
                                  r_den[:, 1, :].unsqueeze(2).broadcast_to([P, TPC * GROUP, KV]),
                                  ALU.mult).then_inc(am_done, 1)

            dve.wait_ge(mw_exp, 1)
            dve.tensor_scalar(mix[:, 2:4], mix[:, 0:2], 1.0, None, ALU.add).then_inc(mix_step, 1)
            dve.wait_ge(mix_step, 1)
            dve.reciprocal(mix[:, 4:6], mix[:, 2:4]).then_inc(mix_step, 1)
            dve.wait_ge(mix_step, 2)
            ffn_moments(f1, 0, 0)

            def phase1(pair, first, last=False):
                for h in range(2):
                    prev = (pair, 0) if h else (pair - 1, 1)
                    has_prev = not (first and h == 0)
                    ffn_hidden(f1, pair, h, 0)
                    if h == 0:
                        ffn_moments(f1, pair, 1)
                    elif not last:
                        ffn_moments(f1, pair + 1, 0)
                    ffn_hidden(f1, pair, h, 1)
                    if has_prev:
                        proj_residues(*prev)
                    ffn_hidden(f1, pair, h, 2)
                    if has_prev:
                        proj_thirds(*prev)
                    ffn_residual(f1, pair, h)
                    proj_moments(pair, h)
                    if has_prev:
                        memory_read(*prev)

            phase1(0, True)
            with dve.Fori(1, CHUNKS // 2 - 1) as pair:
                phase1(pair, False)
            phase1(CHUNKS // 2 - 1, False, True)
            proj_residues(CHUNKS // 2 - 1, 1)
            proj_thirds(CHUNKS // 2 - 1, 1)
            memory_read(CHUNKS // 2 - 1, 1)

            def row_maxima(K, par, st):
                for q in range(2 * GROUP):
                    n = 4 * st + q
                    dve.wait_ge(a_ready, at(32, K, n + 1))
                    dve.tensor_reduce(mx[:, par, q // 2, st, q % 2:q % 2 + 1], a_b[n % 3][:, :], AX.X, ALU.max
                                      ).then_inc(a_used, 1)

            def whole_maxima(K, par):
                dve.wait_ge(a_used, at(32, K, 32))
                dve.tensor_reduce(m16[:, par, :, :], mx[:, par, :, :, :], AX.X, ALU.max).then_inc(m_max, 1)

            def normalise(J):
                dve.wait_ge(o_ps, at(1, J, 1))
                o = misc_b[:, :].rearrange("p (c q e) -> p c q e", c=4, q=4)
                dve.reciprocal(r_sum[:, 0, :, :], o[:, :, :, DH]).then_inc(o_step, 1)
                dve.wait_ge(o_step, at(2, J, 1))
                dve.tensor_scalar(r_sum[:, 1, :, :], r_sum[:, 0, :, :], omw_col, None, ALU.mult).then_inc(o_step, 1)
                dve.wait_ge(o_step, at(2, J, 2))
                if not (isinstance(J, int) and J == 0):
                    dve.wait_ge(xm_added, at(1, J, 0))
                for g in range(GROUP):
                    for half in range(2):
                        q = 2 * g + half
                        i = dve.tensor_tensor(o_n[:, half, :, g, :], o[:, :, q, 0:DH],
                                              r_sum[:, 1, :, q].unsqueeze(2).broadcast_to([P, 4, DH]), ALU.mult)
                i.then_inc(o_norm, 1)

            for st in range(TILES):
                row_maxima(0, 0, st)
            whole_maxima(0, 0)
            for st in range(LEAD):
                row_maxima(1, 1, st)

            def pairs(it, first, last):
                for u in range(SLOTS):
                    J = it * SLOTS + u
                    for i in range(TILES):
                        n, st = ahead(i)
                        if not (last and u + n >= SLOTS):
                            row_maxima(J + n, (u + n) % 2, st)
                            if st == TILES - 1:
                                whole_maxima(J + n, (u + n) % 2)
                        if i == 2 and not (first and u == 0):
                            normalise(J - 1)

            attention_loop(dve, pairs)
            normalise(PAIRS - 1)

            ffn_moments(f3, 0, 0)

            def phase3(pair, last=False):
                for h in range(2):
                    ffn_hidden(f3, pair, h, 0)
                    if h == 0:
                        ffn_moments(f3, pair, 1)
                    elif not last:
                        ffn_moments(f3, pair + 1, 0)
                    ffn_hidden(f3, pair, h, 1)
                    ffn_hidden(f3, pair, h, 2)
                    ffn_residual(f3, pair, h)

            phase3(0)
            with dve.Fori(1, CHUNKS // 2 - 1) as pair:
                phase3(pair)
            phase3(CHUNKS // 2 - 1, True)

        @block.tensor
        def _(pe):
            mm = pe.matmul

            def ffn_transpose(f, pair, h):
                pe.wait_ge(f.xhat, at(2, pair, h + 1))
                if f is f1 and not (isinstance(pair, int) and pair == 0):
                    pe.wait_ge(v_sb, at(2, pair, h - 1))
                for m in range(TPC):
                    i = pe.transpose(tr_b[:, P * m:P * m + P], x_hat[:, h, m, :], ident[:, :])
                i.then_inc(f.xt_ps, 1)

            def ffn_up(f, pair, h, k):
                n = KH * h + k
                if k == 0:
                    pe.wait_ge(f.xt, at(2, pair, h + 1))
                if not isinstance(pair, int) or pair > 0 or n >= 2:
                    pe.wait_ge(f.hidden, at(2 * KH, pair, n - 1))
                mm(gate_b[n % 2][:, :], w_f[:, 0, P * k:P * k + P], x_t[:, h, :], start=True, stop=True)
                mm(up_b[n % 2][:, :], w_f[:, 1, P * k:P * k + P], x_t[:, h, :], start=True, stop=True).then_inc(f.gu, 1)

            def ffn_down(f, pair, h):
                pe.wait_ge(f.hidden, at(2 * KH, pair, KH * h + KH))
                if not (isinstance(pair, int) and pair == 0 and h == 0):
                    pe.wait_ge(f.res, at(2, pair, h))
                for m in range(TPC):
                    for k in range(KH):
                        i = mm(y_b[:, P * m:P * m + P], hid[:, h, k, P * m:P * m + P], w_f[:, 2, P * k:P * k + P],
                               start=(k == 0), stop=(k == KH - 1))
                i.then_inc(f.y, 1)

            def proj_transpose(pair, h):
                pe.wait_ge(xn_ready, at(2, pair, h + 1))
                for m in range(TPC):
                    i = pe.transpose(tr_b[:, P * m:P * m + P], xn_hat[:, m, :], ident[:, :])
                i.then_inc(xn_ps, 1)

            def proj(pair, h):
                pe.wait_ge(xn_sb, at(2, pair, h + 1))
                if not (isinstance(pair, int) and pair == 0 and h == 0):
                    pe.wait_ge(am_done, at(2, pair, h))
                mm(q_b[:, :], wq_s[:, :], xn_t[:, :], start=True, stop=True).then_inc(q_ps, 1)
                mm(k_b[0:KV, :], wk_s[:, :], xn_t[:, :], start=True, stop=True).then_inc(k_ps, 1)
                for m in range(TPC):
                    i = mm(tr_b[:, KV * m:KV * m + KV], xn_t[:, P * m:P * m + P], wv_s[:, :], start=True, stop=True)
                i.then_inc(v_ps, 1)

            def memory_product(pair, h):
                pe.wait_ge(q_elud, at(2, pair, h + 1))
                pe.wait_ge(q3_done, at(2, pair, h + 1))
                pe.wait_ge(k_res, at(2, pair, h + 1))
                for m in range(TPC):
                    mm(q_b[:, P * m:P * m + P], q_elu[:, P * m:P * m + P], mem_s[:, :], start=True, stop=True)
                    i = mm(k_b[:, GROUP * m:GROUP * (m + 1)], q_elu[:, P * m:P * m + P], norm_s[:, :],
                           start=True, stop=True)
                i.then_inc(am_ps, 1)

            pe.wait_ge(ident_set, 3)
            pe.wait_ge(w_cast, 1)

            def phase1(pair, first):
                for h in range(2):
                    prev = (pair, 0) if h else (pair - 1, 1)
                    has_prev = not (first and h == 0)
                    ffn_transpose(f1, pair, h)
                    ffn_up(f1, pair, h, 0)
                    if has_prev:
                        if first:
                            pe.wait_ge(mem_loaded, 16 * 7)
                        proj_transpose(*prev)
                    ffn_up(f1, pair, h, 1)
                    if has_prev:
                        proj(*prev)
                    ffn_up(f1, pair, h, 2)
                    ffn_down(f1, pair, h)
                    if has_prev:
                        memory_product(*prev)

            chunk_loop(pe, phase1)
            proj_transpose(CHUNKS // 2 - 1, 1)
            proj(CHUNKS // 2 - 1, 1)
            memory_product(CHUNKS // 2 - 1, 1)

            def max_scores(it, u, J, n, st, q):
                K, slot = J + n, (u + n) % SLOTS
                idx = 4 * st + q
                if idx == 0:
                    pe.wait_ge(loaded[slot], at(LOADS * 16, it + (u + n) // SLOTS, LOADS * 16))
                if not (isinstance(K, int) and K == 0 and idx < 3):
                    pe.wait_ge(a_used, at(32, K, (-1, 0, -2)[idx] if idx < 3 else idx - 2))
                g, half = q // 2, q % 2
                mm(a_b[idx % 3][:, :], q_op[0:MAXROW, slot, g, P * st:P * st + P],
                   k_op[0:MAXROW, slot, 512 * half:512 * half + 512], start=True, stop=True).then_inc(a_ready, 1)

            def scores(J, u, i, q):
                idx = 4 * i + q
                if idx == 0:
                    pe.wait_ge(m_in, at(2 * PARTS * 16, J, 2 * PARTS * 16))
                if not (isinstance(J, int) and J == 0 and idx < 3):
                    pe.wait_ge(p_ready, at(32, J, (-1, 0, -2)[idx] if idx < 3 else idx - 2))
                g, half = q // 2, q % 2
                mm(t_b[idx % 3][:, :], k_op[0:MAXROW + PARTS, u, P * i:P * i + P],
                   q_op[0:MAXROW + PARTS, u, g, 512 * half:512 * half + 512], start=True, stop=True
                   ).then_inc(t_ready, 1)

            def weigh_values(J, par, i):
                pe.wait_ge(p_ready, at(32, J, 4 * i + 4))
                if i == 0:
                    pe.wait_ge(v9_ready, at(1, J, 1))
                    if not (isinstance(J, int) and J == 0):
                        pe.wait_ge(pv_sb, at(1, J, 0))
                for q in range(2 * GROUP):
                    m = mm(pv_b[VPAD * q:VPAD * q + VPAD, :], v9[:, par, i, :], probs[:, i % 2, q, :],
                           start=(i == 0), stop=(i == TILES - 1))
                if i == TILES - 1:
                    m.then_inc(pv_done, 1)

            def transpose_max(K, par):
                if not (isinstance(K, int) and K < 2):
                    pe.wait_ge(o_norm, at(1, K, -1))
                wait_alone(pe, m_split, at(5, K, 5))
                pe.transpose(misc_b[:, :].bitcast(bf16)[0:MCOLS, 0:P],
                             m_parts[:, par, :, :, :].rearrange("p g a t -> p (g a t)"), ident_b[:, :]
                             ).then_inc(m_ps, 1)

            def transpose_sums(J, par):
                pe.wait_ge(pv_sb, at(1, J, 1))
                if not (isinstance(J, int) and J == PAIRS - 1):
                    pe.wait_ge(m_sb, at(1, J, 2))
                else:
                    pe.wait_ge(o_norm, PAIRS - 1)
                for c in range(4):
                    i = pe.transpose(misc_b[:, P * c:P * c + P], o_t[:, par, P * c:P * c + P], ident[:, :])
                i.then_inc(o_ps, 1)

            pe.wait_ge(am_done, CHUNKS)
            pe.wait_ge(v_sb, CHUNKS)
            for st in range(TILES):
                for q in range(2 * GROUP):
                    max_scores(0, 0, 0, 0, st, q)
            for st in range(LEAD):
                for q in range(2 * GROUP):
                    max_scores(0, 0, 0, 1, st, q)
            transpose_max(0, 0)

            def pairs(it, first, last):
                for u in range(SLOTS):
                    J = it * SLOTS + u
                    for i in range(TILES):
                        n, st = ahead(i)
                        if i == 2 and not (first and u == 0):
                            transpose_sums(J - 1, (u - 1) % 2)
                        if i == 6 and not (last and u == SLOTS - 1):
                            transpose_max(J + 1, (u + 1) % 2)
                        for q in range(2 * GROUP):
                            scores(J, u, i, q)
                            if not (last and u + n >= SLOTS):
                                max_scores(it, u, J, n, st, q)
                        if i > 0:
                            weigh_values(J, u % 2, i - 1)
                        elif not (first and u == 0):
                            weigh_values(J - 1, (u - 1) % 2, TILES - 1)

            attention_loop(pe, pairs)
            weigh_values(PAIRS - 1, 1, TILES - 1)
            transpose_sums(PAIRS - 1, 1)

            def phase3(pair):
                for h in range(2):
                    ffn_transpose(f3, pair, h)
                    for k in range(KH):
                        ffn_up(f3, pair, h, k)
                    ffn_down(f3, pair, h)

            phase3(0)
            with pe.Fori(1, CHUNKS // 2) as pair:
                phase3(pair)


def kernel(L0_attn_x, L0_attn_Wq, L0_attn_Wk, L0_attn_Wv, L0_attn_memory, L0_attn_memory_norm,
           L0_attn_memory_weight, L0_ffn_w_gate, L0_ffn_w_up, L0_ffn_w_down):
    import numpy as np
    import concourse.bacc as bacc
    from concourse.bass_utils import run_bass_kernel_spmd

    arrays = {
        "x": L0_attn_x, "wq": L0_attn_Wq, "wk": L0_attn_Wk, "wv": L0_attn_Wv, "memory": L0_attn_memory,
        "memory_norm": L0_attn_memory_norm, "memory_weight": L0_attn_memory_weight,
        "wg_t": np.asarray(L0_ffn_w_gate).T, "wu_t": np.asarray(L0_ffn_w_up).T, "wd_t": np.asarray(L0_ffn_w_down).T,
    }
    arrays = {n: np.ascontiguousarray(a) for n, a in arrays.items()}
    nc = bacc.Bacc("TRN2", target_bir_lowering=False, num_devices=1)
    args = [nc.dram_tensor(n, a.shape, mybir.dt.from_np(a.dtype), kind="ExternalInput").ap()
            for n, a in arrays.items()]
    out = nc.dram_tensor("out", (B, S, D), mybir.dt.float32, kind="ExternalOutput").ap()
    build(nc, *args, out)
    run = run_bass_kernel_spmd(nc, [arrays], core_ids=[0])
    return run.results[0]["out"]
```

```python
from contextlib import ExitStack

import concourse.bass as bass
from concourse import mybir

P = 128
B, S, D = 4, 1024, 128
HEADS_KV, GROUP, DH = 8, 2, 8
KV = HEADS_KV * DH
HID = 384
KH = HID // P
CH = 512
TPC = CH // P
CHUNKS = B * S // CH
TILES = S // P
PAIRS = B * HEADS_KV
PARTS = 3
QROWS = PARTS * PARTS * DH
MAXROW = 96
SLOTS = 4
LEAD = 3
LN_EPS = 1e-5
FFN_SCALE = 1.0 / 127.0
TANH_SCALE = 0.5 * FFN_SCALE
Y_SCALE = 0.5 * 0.5 * FFN_SCALE ** 3
SM_SCALE = float(DH) ** -0.5
VW = DH + 1
VPAD = 32
MCOLS = GROUP * PARTS * TILES


def build(nc, x, wq, wk, wv, memory, memory_norm, memory_weight, wg_t, wu_t, wd_t, out):
    f32, bf16, i32 = mybir.dt.float32, mybir.dt.bfloat16, mybir.dt.int32
    ALU, ACT, AX = mybir.AluOpType, mybir.ActivationFunctionType, mybir.AxisListType

    q_spill = nc.dram_tensor("q_spill", [PAIRS * GROUP * DH, PARTS, S], bf16, kind="Internal").ap()
    k_spill = nc.dram_tensor("k_spill", [PAIRS * DH, PARTS, S], bf16, kind="Internal").ap()
    x_rows = x.rearrange("b (t p) d -> p (b t) d", p=P)
    out_rows = out.rearrange("b (t p) d -> p (b t) d", p=P)

    ctx = ExitStack()
    with ctx:
        def sb(name, shape, dt=f32):
            return ctx.enter_context(nc.sbuf_tensor(name, shape, dt))

        def bank(name):
            return ctx.enter_context(nc.psum_tensor(name, [P, 512], f32))

        def sem(name):
            return ctx.enter_context(nc.semaphore(name))

        ident = sb("ident", [P, P])
        ident_b = sb("ident_b", [P, P], bf16)
        wq_s, wk_s, wv_s = sb("wq_s", [P, D]), sb("wk_s", [P, KV]), sb("wv_s", [P, KV])
        mem_s = sb("mem_s", [P, D])
        norm_s = sb("norm_s", [P, GROUP])
        w_int = sb("w_int", [P, 3, HID], i32)
        w_f = sb("w_f", [P, 3, HID])
        mw = sb("mw", [P, 1])
        mix = sb("mix", [P, 6])
        w_col, omw_col = mix[:, 4:5], mix[:, 5:6]
        x_n = sb("x_n", [P, 2, TPC, D])
        x_r = sb("x_r", [P, 2, TPC, D])
        st6 = sb("st6", [P, 2, TPC, 6])
        mv = sb("mv", [P, 2, TPC, 2])
        rstd = sb("rstd", [P, 2, 4, TPC])
        neg_half, neg_one = sb("neg_half", [P, TPC]), sb("neg_one", [P, TPC])
        x_hat = sb("x_hat", [P, 2, TPC, D])
        x_t = sb("x_t", [P, 2, CH])
        th = sb("th", [P, 2, CH])
        gated = sb("gated", [P, 2, CH])
        hid = sb("hid", [P, 2, KH, CH])
        out_c = sb("out_c", [P, 2, TPC, D])
        x1_c = sb("x1_c", [P, 2, TPC, D])
        st6b = sb("st6b", [P, TPC, 6])
        mvb = sb("mvb", [P, TPC, 2])
        rstdb = sb("rstdb", [P, 4, TPC])
        xn_hat = sb("xn_hat", [P, TPC, D])
        xn_t = sb("xn_t", [P, CH])
        q_p = sb("q_p", [P, 2, PARTS, CH], bf16)
        k_p = sb("k_p", [KV, 2, PARTS, CH], bf16)
        q_r, k_r = sb("q_r", [P, CH]), sb("k_r", [KV, CH])
        q_neg, q_exp, q_elu = sb("q_neg", [P, CH]), sb("q_exp", [P, CH]), sb("q_elu", [P, CH])
        r_den = sb("r_den", [P, 2, TPC * GROUP])
        a_mem = sb("a_mem", [P, TPC, D])
        v_all = sb("v_all", [P, PAIRS, TILES * VW])
        xm = sb("xm", [P, PAIRS, TILES, GROUP * DH])
        q_op = sb("q_op", [P, SLOTS, GROUP, S], bf16)
        k_op = sb("k_op", [P, SLOTS, S], bf16)
        mx = sb("mx", [P, 2, GROUP, TILES, 2])
        m16 = sb("m16", [P, 2, GROUP, TILES])
        m_neg, m_res = sb("m_neg", [P, GROUP, TILES]), sb("m_res", [P, GROUP, TILES])
        m_parts = sb("m_parts", [P, 2, PARTS, GROUP, TILES], bf16)
        m_rows = sb("m_rows", [MCOLS, 2, P], bf16)
        probs = sb("probs", [P, 2, 2 * GROUP, 512])
        v9 = sb("v9", [P, 2, TILES, VPAD])
        o_t = sb("o_t", [P, 2, 512])
        o_s = sb("o_s", [P, 2, 4, 4, VW])
        r_sum = sb("r_sum", [P, 2, 4, 4])
        r_mix = sb("r_mix", [P, 4, 4])
        omw_16 = sb("omw_16", [P, 4, 4])
        o_n = sb("o_n", [P, 4, 4, DH])

        banks = [bank(f"bank{n}") for n in range(8)]
        gate_b, up_b = (banks[0], banks[2]), (banks[1], banks[3])
        tr_b, y_b, q_b, k_b = banks[4], banks[5], banks[6], banks[7]
        a_b, t_b, pv_b, misc_b = banks[0:3], banks[3:6], banks[6], banks[7]

        xn_in, xr_in = [sem("xn_in0"), sem("xn_in1")], [sem("xr_in0"), sem("xr_in1")]
        w_loaded = sem("w_loaded")
        mem_loaded, mw_loaded = sem("mem_loaded"), sem("mw_loaded")
        zeroed, ones_set, ident_set, op_set = sem("zeroed"), sem("ones_set"), sem("ident_set"), sem("op_set")
        w_cast, mw_exp, mix_step = sem("w_cast"), sem("mw_exp"), sem("mix_step")

        class FfnSems:
            def __init__(self, tag):
                self.src, self.ln, self.root, self.xhat = (sem(f"{tag}_{n}") for n in ("src", "ln", "root", "xhat"))
                self.scale = sem(f"{tag}_scale")
                self.xt_ps, self.xt, self.gu, self.th = (sem(f"{tag}_{n}") for n in ("xt_ps", "xt", "gu", "th"))
                self.gated, self.hidden, self.y, self.res = (
                    sem(f"{tag}_{n}") for n in ("gated", "hidden", "y", "res"))

        f1, f3 = FfnSems("ffn1"), FfnSems("ffn2")
        ln2, root2, scale2 = sem("ln2"), sem("root2"), sem("scale2")
        xn_ready, xn_ps, xn_sb = sem("xn_ready"), sem("xn_ps"), sem("xn_sb")
        q_ps, k_ps, v_ps, v_sb = sem("q_ps"), sem("k_ps"), sem("v_ps"), sem("v_sb")
        q1_done, q_res, q2_done, q3_done = sem("q1_done"), sem("q_res"), sem("q2_done"), sem("q3_done")
        k1_done, k_res, k2_done, k3_done = sem("k1_done"), sem("k_res"), sem("k2_done"), sem("k3_done")
        q_min, q_expd, q_elud, am_ps = sem("q_min"), sem("q_expd"), sem("q_elud"), sem("am_ps")
        am_step, am_done, xm_done = sem("am_step"), sem("am_done"), sem("xm_done")
        spilled = [sem("spilled0"), sem("spilled1")]
        loaded = [sem(f"loaded{s}") for s in range(SLOTS)]
        a_ready, a_used, m_max, m_split, m_ps, m_sb, m_in = (
            sem(n) for n in ("a_ready", "a_used", "m_max", "m_split", "m_ps", "m_sb", "m_in"))
        t_ready, p_ready, pv_done, pv_sb = (sem(n) for n in ("t_ready", "p_ready", "pv_done", "pv_sb"))
        v9_ready, o_ps, o_sb, o_rec, o_norm, xm_added = (
            sem(n) for n in ("v9_ready", "o_ps", "o_sb", "o_rec", "o_norm", "xm_added"))
        stored = [sem("stored0"), sem("stored1")]
        waits_passed = sem("waits_passed")
        CREDIT = 16
        LOADS = GROUP + PARTS
        block = ctx.enter_context(nc.Block())

        def at(n, c, k):
            return c * n + k

        def chunk(pair, h, k):
            d, h = divmod(h + k, 2)
            there = not isinstance(pair, int) or 0 <= 2 * (pair + d) + h < CHUNKS
            return (pair + d, h) if there else None

        def do(step, pair, h, k, *more):
            c = chunk(pair, h, k)
            if c is not None:
                step(*c, *more)

        def later(pair, h, n):
            return not isinstance(pair, int) or 2 * pair + h >= n

        def chunk_loop(eng, body):
            for pair in (-1, 0):
                body(pair, 0)
                body(pair, 1)
            with eng.Fori(1, CHUNKS // 2 - 1) as pair:
                body(pair, 0)
                body(pair, 1)
            body(CHUNKS // 2 - 1, 0)
            body(CHUNKS // 2 - 1, 1)

        def phase3_loop(eng, body):
            body(0, 0)
            body(0, 1)
            with eng.Fori(1, CHUNKS // 2 - 1) as pair:
                body(pair, 0)
                body(pair, 1)
            body(CHUNKS // 2 - 1, 0)
            body(CHUNKS // 2 - 1, 1)

        def attention_loop(eng, body, before_last=None):
            body(0, True, False)
            with eng.Fori(1, PAIRS // SLOTS - 1) as it:
                body(it, False, False)
            if before_last:
                before_last()
            body(PAIRS // SLOTS - 1, False, True)

        def wait_alone(eng, semaphore, count):
            eng.wait_ge(semaphore, count)
            if not isinstance(count, int):
                eng.sem_inc(waits_passed, 1)

        def ahead(i):
            return (1, i + LEAD) if i + LEAD < TILES else (2, i + LEAD - TILES)

        @block.sync
        def _(sp):
            def rows_of(pair, h):
                return x_rows[:, bass.ds(pair * (2 * TPC) + h * TPC, TPC), :]

            def load_n(pair, h):
                if later(pair, h, 2):
                    sp.wait_ge(f1.xhat, at(2, pair, h - 1))
                sp.dma_start(x_n[:, h, :, :], rows_of(pair, h)).then_inc(xn_in[h], 16)

            def load_r(pair, h):
                if later(pair, h, 2):
                    sp.wait_ge(f1.res, at(2, pair, h - 1))
                sp.dma_start(x_r[:, h, :, :], rows_of(pair, h)).then_inc(xr_in[h], 16)

            def load_pair(J, slot):
                R = DH * PARTS
                for g in range(GROUP):
                    v = q_spill[bass.ds(J * (GROUP * DH) + g * DH, DH), :, :]
                    sp.dma_start(q_op[0:QROWS, slot, g, :],
                                 bass.AP(v.tensor, v.offset, [[0, PARTS], [S, R], [1, S]])).then_inc(loaded[slot], 16)
                for a in range(PARTS):
                    v = k_spill[bass.ds(J * DH, DH), a, :]
                    sp.dma_start(k_op[R * a:R * a + R, slot, :],
                                 bass.AP(v.tensor, v.offset, [[PARTS * S, DH], [0, PARTS], [1, S]])
                                 ).then_inc(loaded[slot], 16)

            def spill(pair, h):
                sp.wait_ge(q3_done, at(2, pair, h + 1))
                sp.dma_start(q_spill[bass.ds(pair * P, P), :, h * CH:(h + 1) * CH],
                             q_p[:, h, :, :]).then_inc(spilled[h], 16)
                sp.wait_ge(k3_done, at(2, pair, h + 1))
                sp.dma_start(k_spill[bass.ds(pair * KV, KV), :, h * CH:(h + 1) * CH],
                             k_p[:, h, :, :]).then_inc(spilled[h], 16)

            def phase1(pair, h):
                do(load_n, pair, h, 2)
                do(spill, pair, h, -2)
                do(load_r, pair, h, 1)

            chunk_loop(sp, phase1)
            sp.wait_ge(op_set, 2)
            for h in range(2):
                sp.wait_ge(spilled[h], CREDIT + 32)
            for s in range(SLOTS - 1):
                load_pair(s, s)
            spill(CHUNKS // 2 - 1, 0)
            spill(CHUNKS // 2 - 1, 1)

            def m_to_operand(K, slot, par):
                sp.wait_ge(m_sb, at(1, K, 1))
                sp.dma_start(q_op[MAXROW:MAXROW + PARTS, slot, :, :].rearrange("a g (t p) -> a (g t) p", p=P),
                             m_rows[:, par, :]).then_inc(m_in, 16)

            m_to_operand(0, 0, 0)
            for h in range(2):
                sp.wait_ge(spilled[h], CREDIT + 32 * B)

            def pairs(it, first, last):
                for u in range(SLOTS):
                    J = it * SLOTS + u
                    if not (last and u > 0):
                        if not (first and u == 0):
                            sp.wait_ge(t_ready, at(32, J, 0))
                        load_pair(J + SLOTS - 1, (u + SLOTS - 1) % SLOTS)
                    if not (last and u == SLOTS - 1):
                        m_to_operand(J + 1, (u + 1) % SLOTS, (u + 1) % 2)

            attention_loop(sp, pairs)

            def store(pair, h):
                sp.wait_ge(f3.res, at(2, pair, h + 1))
                sp.dma_start(out_rows[:, bass.ds(pair * (2 * TPC) + h * TPC, TPC), :],
                             out_c[:, h, :, :]).then_inc(stored[h], 16)

            with sp.Fori(0, CHUNKS // 2) as pair:
                store(pair, 0)
                store(pair, 1)
            for h in range(2):
                sp.wait_ge(stored[h], 16 * (CHUNKS // 2))

        @block.gpsimd
        def _(pool):
            for h in range(2):
                pool.sem_inc(spilled[h], CREDIT)
            pool.memset(neg_half[:, :], -0.5)
            pool.memset(neg_one[:, :], -1.0)
            pool.memset(mem_s[:, :], 0.0)
            pool.memset(norm_s[:, :], 0.0).then_inc(zeroed, 1)
            pool.memset(ident[:, :], 0.0)
            pool.memset(ident_b[:, :], 0.0).then_inc(ident_set, 1)
            pool.wait_ge(ident_set, 1)
            for m in (ident, ident_b):
                pool.affine_select(out=m[:, :], in_=m[:, :], compare_op=ALU.not_equal, fill=1.0, base=0,
                                   pattern=[[-1, P]], channel_multiplier=1).then_inc(ident_set, 1)

            def x1_plus_memory(pair, h):
                wait_alone(pool, am_done, at(2, pair, h + 1))
                dst = xm[:, bass.ds(pair * HEADS_KV, HEADS_KV), h * TPC:(h + 1) * TPC, :]
                for m in range(TPC):
                    i = pool.tensor_tensor(
                        dst[:, :, m, :], a_mem[:, m, :].rearrange("p (j e) -> p j e", j=HEADS_KV),
                        x1_c[:, h, m, :].rearrange("p (j e) -> p j e", j=HEADS_KV), ALU.add)
                i.then_inc(xm_done, 1)

            def scale_and_bias(agg, rs, steps, n, ready):
                pool.tensor_scalar(rs[:, 0, :], agg[:, :, 1], LN_EPS, None, ALU.add)
                pool.tensor_tensor(rs[:, 2, :], agg[:, :, 0], neg_one[:, :], ALU.mult).then_inc(steps, 1)
                wait_alone(pool, steps, n + 1)
                pool.tensor_tensor(rs[:, 1, :], rs[:, 0, :], neg_half[:, :], ALU.pow).then_inc(steps, 1)
                wait_alone(pool, steps, n + 2)
                pool.tensor_tensor(rs[:, 3, :], rs[:, 2, :], rs[:, 1, :], ALU.mult).then_inc(ready, 1)

            def ffn_scale(f, pair, h):
                wait_alone(pool, f.ln, at(4, pair, 2 * h + 2))
                scale_and_bias(mv[:, h, :, :], rstd[:, h, :, :], f.root, at(4, pair, 2 * h), f.scale)

            def ffn1_scale(pair, h):
                ffn_scale(f1, pair, h)

            def proj_scale(pair, h):
                wait_alone(pool, ln2, at(4, pair, 2 * h + 2))
                scale_and_bias(mvb, rstdb, root2, at(4, pair, 2 * h), scale2)

            def phase1(pair, h):
                do(proj_scale, pair, h, -1)
                do(ffn1_scale, pair, h, 2)
                do(x1_plus_memory, pair, h, -2)

            for pair in (-1, 0):
                phase1(pair, 0)
                phase1(pair, 1)
                if pair < 0:
                    pool.memset(v_all[:, :, :], 1.0).then_inc(ones_set, 1)
            pool.memset(v9[:, :, :, :], 0.0)
            pool.memset(q_op[:, :, :, :], 0.0)
            pool.memset(k_op[:, :, :], 0.0).then_inc(op_set, 1)
            pool.wait_ge(op_set, 1)
            pool.memset(k_op[MAXROW:P, :, :], 1.0).then_inc(op_set, 1)
            pool.wait_ge(op_set, 2)
            with pool.Fori(1, CHUNKS // 2 - 1) as pair:
                phase1(pair, 0)
                phase1(pair, 1)
            for h in range(4):
                phase1(CHUNKS // 2 - 1 + h // 2, h % 2)

            def split_max(K, par):
                wait_alone(pool, m_max, at(1, K, 1))
                pool.tensor_scalar(m_neg[:, :, :], m16[:, par, :, :], -1.0, None, ALU.mult).then_inc(m_split, 1)
                wait_alone(pool, m_split, at(5, K, 1))
                pool.tensor_copy(m_parts[:, par, 0, :, :], m_neg[:, :, :]).then_inc(m_split, 1)
                wait_alone(pool, m_split, at(5, K, 2))
                pool.tensor_tensor(m_res[:, :, :], m_neg[:, :, :], m_parts[:, par, 0, :, :],
                                   ALU.subtract).then_inc(m_split, 1)
                wait_alone(pool, m_split, at(5, K, 3))
                pool.tensor_copy(m_parts[:, par, 1, :, :], m_res[:, :, :]).then_inc(m_split, 1)
                wait_alone(pool, m_split, at(5, K, 4))
                pool.tensor_tensor(m_parts[:, par, 2, :, :], m_res[:, :, :], m_parts[:, par, 1, :, :],
                                   ALU.subtract).then_inc(m_split, 1)

            def values(J, par):
                pool.tensor_copy(v9[:, par, :, 0:VW], v_all[:, J, :].rearrange("p (t e) -> p t e", t=TILES)
                                 if isinstance(J, int) else
                                 v_all[:, bass.ds(J, 1), :].rearrange("p a (t e) -> p (a t) e", t=TILES)
                                 ).then_inc(v9_ready, 1)

            def add_attention(J, par):
                wait_alone(pool, o_rec, at(1, J, 1))
                pool.tensor_tensor(r_mix[:, :, :], r_sum[:, par, :, :], omw_16[:, :, :], ALU.mult).then_inc(o_norm, 1)
                wait_alone(pool, o_norm, at(2, J, 1))
                pool.tensor_tensor(o_n[:, :, :, :], o_s[:, par, :, :, 0:DH],
                                   r_mix[:, :, :].unsqueeze(3).broadcast_to([P, 4, 4, DH]), ALU.mult
                                   ).then_inc(o_norm, 1)
                wait_alone(pool, o_norm, at(2, J, 2))
                for g in range(GROUP):
                    dst = xm[:, bass.ds(J, 1), :, DH * g:DH * g + DH].rearrange("p a (h c) d -> p (a h) c d", h=2)
                    i = pool.tensor_tensor(dst, dst, o_n[:, :, 2 * g:2 * g + 2, :].rearrange("p c h d -> p h c d"),
                                           ALU.add)
                i.then_inc(xm_added, 1)

            wait_alone(pool, v_sb, CHUNKS)
            values(0, 0)
            split_max(0, 0)

            def pairs(it, first, last):
                for u in range(SLOTS):
                    J = it * SLOTS + u
                    if not (last and u == SLOTS - 1):
                        if not (first and u == 0):
                            wait_alone(pool, pv_done, at(1, J, 0))
                        values(J + 1, (u + 1) % 2)
                    if not (first and u == 0):
                        add_attention(J - 1, (u - 1) % 2)
                    if not (last and u == SLOTS - 1):
                        split_max(J + 1, (u + 1) % 2)

            def before_last():
                gather_x2(0, 0)
                gather_x2(0, 1)
                ffn_scale(f3, 0, 0)
                ffn_scale(f3, 0, 1)


            def gather_x2(pair, h):
                if later(pair, h, 2):
                    wait_alone(pool, f3.xhat, at(2, pair, h - 1))
                wait_alone(pool, xm_added, at(HEADS_KV, pair, HEADS_KV))
                src = xm[:, bass.ds(pair * HEADS_KV, HEADS_KV), h * TPC:(h + 1) * TPC, :]
                for m in range(TPC):
                    i = pool.tensor_copy(x_n[:, h, m, :].rearrange("p (j e) -> p j e", j=HEADS_KV), src[:, :, m, :])
                i.then_inc(f3.src, 1)

            attention_loop(pool, pairs, before_last)
            add_attention(PAIRS - 1, 1)

            def phase3(pair):
                for h in range(2):
                    gather_x2(pair, h)
                    ffn_scale(f3, pair, h)

            with pool.Fori(1, CHUNKS // 2) as pair:
                phase3(pair)

        @block.scalar
        def _(act):
            act.dma_start(mw[:, :], bass.AP(memory_weight.tensor, memory_weight.offset, [[0, P], [1, 1]])
                          ).then_inc(mw_loaded, 16)
            for n, w in enumerate((wg_t, wu_t)):
                act.dma_start(w_int[:, n, :], w).then_inc(w_loaded, 16)
            act.dma_start(w_int[:, 2, :].rearrange("p (k d) -> p k d", k=KH),
                          wd_t.rearrange("(k p) d -> p k d", p=P)).then_inc(w_loaded, 16)
            act.dma_start(wq_s[:, :], wq).then_inc(mem_loaded, 16)
            act.dma_start(wk_s[:, :], wk).then_inc(mem_loaded, 16)
            act.dma_start(wv_s[:, :], wv).then_inc(mem_loaded, 16)
            act.wait_ge(zeroed, 1)
            for g in range(GROUP):
                act.dma_start(mem_s[KV * g:KV * g + KV, KV * g:KV * g + KV], memory).then_inc(mem_loaded, 16)
                act.dma_start(norm_s[KV * g:KV * g + KV, g:g + 1],
                              memory_norm.rearrange("(n a) -> n a", a=1)).then_inc(mem_loaded, 16)
            act.wait_ge(mw_loaded, 16)
            act.activation(mix[:, 0:1], mw[:, :], ACT.Exp, scale=-1.0)
            act.activation(mix[:, 1:2], mw[:, :], ACT.Exp).then_inc(mw_exp, 1)
            act.wait_ge(w_loaded, 16 * 3)
            act.activation(w_f[:, :, :], w_int[:, :, :], ACT.Copy).then_inc(w_cast, 1)

            def normalise(src, dst, rs, ready):
                for m in range(TPC):
                    i = act.activation(dst[:, m, :], src[:, m, :], ACT.Identity, bias=rs[:, 3, m:m + 1],
                                       scale=rs[:, 1, m:m + 1])
                i.then_inc(ready, 1)

            def ffn_normalise(f, pair, h):
                act.wait_ge(f.scale, at(2, pair, h + 1))
                if later(pair, h, 2):
                    act.wait_ge(f.xt_ps, at(2, pair, h - 1))
                normalise(x_n[:, h, :, :], x_hat[:, h, :, :], rstd[:, h, :, :], f.xhat)

            def proj_normalise(pair, h):
                act.wait_ge(scale2, at(2, pair, h + 1))
                if later(pair, h, 1):
                    act.wait_ge(xn_ps, at(2, pair, h))
                normalise(x1_c[:, h, :, :], xn_hat, rstdb, xn_ready)

            def ffn_xt(f, pair, h):
                act.wait_ge(f.xt_ps, at(2, pair, h + 1))
                act.activation(x_t[:, h, :], tr_b[:, :], ACT.Copy).then_inc(f.xt, 1)

            def ffn_tanh(f, pair, h, k):
                n = KH * h + k
                act.wait_ge(f.gu, at(2 * KH, pair, n + 1))
                if later(pair, h, 1) or k == 2:
                    act.wait_ge(f.hidden, at(2 * KH, pair, n - 1))
                act.activation(th[:, n % 2, :], gate_b[n % 2][:, :], ACT.Tanh, scale=TANH_SCALE).then_inc(f.th, 1)

            def proj_xn(pair, h):
                act.wait_ge(xn_ps, at(2, pair, h + 1))
                act.activation(xn_t[:, :], tr_b[:, :], ACT.Copy).then_inc(xn_sb, 1)

            def proj_first(pair, h):
                act.wait_ge(spilled[h], at(32, pair, CREDIT))
                act.wait_ge(q_ps, at(2, pair, h + 1))
                act.activation(q_p[:, h, 0, :], q_b[:, :], ACT.Copy).then_inc(q1_done, 1)
                act.wait_ge(k_ps, at(2, pair, h + 1))
                act.activation(k_p[:, h, 0, :], k_b[0:KV, :], ACT.Copy).then_inc(k1_done, 1)
                act.wait_ge(v_ps, at(2, pair, h + 1))
                if isinstance(pair, int) and pair == 0 and h == 0:
                    act.wait_ge(ones_set, 1)
                for m in range(TPC):
                    o = (h * TPC + m) * VW
                    i = act.activation(v_all[:, bass.ds(pair * HEADS_KV, HEADS_KV), o:o + DH],
                                       tr_b[:, KV * m:KV * m + KV].rearrange("p (j d) -> p j d", d=DH), ACT.Copy)
                i.then_inc(v_sb, 1)

            def proj_second(pair, h):
                act.wait_ge(q_min, at(2, pair, h + 1))
                act.activation(q_exp[:, :], q_neg[:, :], ACT.Exp).then_inc(q_expd, 1)
                act.wait_ge(q_res, at(2, pair, h + 1))
                act.activation(q_p[:, h, 1, :], q_r[:, :], ACT.Copy).then_inc(q2_done, 1)
                act.wait_ge(k_res, at(2, pair, h + 1))
                act.activation(k_p[:, h, 1, :], k_r[:, :], ACT.Copy).then_inc(k2_done, 1)

            def phase1(pair, h):
                do(lambda *c: ffn_tanh(f1, *c, 1), pair, h, 0)
                do(lambda *c: ffn_xt(f1, *c), pair, h, 1)
                do(lambda *c: ffn_tanh(f1, *c, 2), pair, h, 0)
                do(proj_normalise, pair, h, -1)
                do(lambda *c: ffn_tanh(f1, *c, 0), pair, h, 1)
                do(proj_xn, pair, h, -1)
                do(lambda *c: ffn_normalise(f1, *c), pair, h, 2)
                do(proj_first, pair, h, -1)
                do(proj_second, pair, h, -1)

            chunk_loop(act, phase1)
            phase1(CHUNKS // 2, 0)

            def max_rows(K, par):
                act.wait_ge(m_ps, at(1, K, 1))
                act.activation(m_rows[:, par, :], misc_b[:, :].bitcast(bf16)[0:MCOLS, 0:P], ACT.Copy
                               ).then_inc(m_sb, 1)

            def sums_out(J, par):
                act.wait_ge(o_ps, at(1, J, 1))
                act.activation(o_s[:, par, :, :, :],
                               misc_b[:, :].rearrange("p (c q e) -> p c q e", c=4, q=4)[:, :, :, 0:VW],
                               ACT.Copy).then_inc(o_sb, 1)

            def pv_out(J, par):
                act.wait_ge(pv_done, at(1, J, 1))
                act.activation(o_t[:, par, :], pv_b[:, :], ACT.Copy).then_inc(pv_sb, 1)

            max_rows(0, 0)

            def pairs(it, first, last):
                for u in range(SLOTS):
                    J = it * SLOTS + u
                    for i in range(TILES):
                        for q in range(2 * GROUP):
                            act.wait_ge(t_ready, at(32, J, 4 * i + q + 1))
                            act.activation(probs[:, i % 2, q, :], t_b[(4 * i + q) % 3][:, :], ACT.Exp,
                                           scale=SM_SCALE).then_inc(p_ready, 1)
                            if i == 2 and q == 1 and not (first and u == 0):
                                sums_out(J - 1, (u - 1) % 2)
                            if i == 6 and q == 1 and not (last and u == SLOTS - 1):
                                max_rows(J + 1, (u + 1) % 2)
                        if i == 0 and not (first and u == 0):
                            pv_out(J - 1, (u - 1) % 2)

            def before_last():
                ffn_normalise(f3, 0, 0)
                ffn_normalise(f3, 0, 1)

            attention_loop(act, pairs, before_last)
            ffn_xt(f3, 0, 0)
            pv_out(PAIRS - 1, 1)
            ffn_tanh(f3, 0, 0, 0)
            sums_out(PAIRS - 1, 1)

            def phase3(pair, h):
                ffn_tanh(f3, pair, h, 1)
                do(lambda *c: ffn_xt(f3, *c), pair, h, 1)
                ffn_tanh(f3, pair, h, 2)
                do(lambda *c: ffn_normalise(f3, *c), pair, h, 2)
                do(lambda *c: ffn_tanh(f3, *c, 0), pair, h, 1)

            phase3_loop(act, phase3)

        @block.vector
        def _(dve):
            def moments(src, s6, agg, steps, n):
                for m in range(TPC):
                    i = dve.bn_stats(s6[:, m, :], src(m))
                i.then_inc(steps, 1)
                wait_alone(dve, steps, n + 1)
                for m in range(TPC):
                    i = dve.bn_aggr(agg[:, m, :], s6[:, m, :])
                i.then_inc(steps, 1)

            def ffn_moments(f, pair, h):
                if later(pair, h, 2):
                    dve.wait_ge(f.xhat, at(2, pair, h - 1))
                if f is f1:
                    dve.wait_ge(xn_in[h], at(16, pair, 16))
                else:
                    dve.wait_ge(f.src, at(2, pair, h + 1))
                moments(lambda m: x_n[:, h, m, :], st6[:, h, :, :], mv[:, h, :, :], f.ln, at(4, pair, 2 * h))

            def ffn_hidden(f, pair, h, k):
                n = KH * h + k
                dve.wait_ge(f.th, at(2 * KH, pair, n + 1))
                dve.scalar_tensor_tensor(gated[:, n % 2, :], th[:, n % 2, :], 1.0, gate_b[n % 2][:, :],
                                         ALU.add, ALU.mult).then_inc(f.gated, 1)
                dve.wait_ge(f.gated, at(2 * KH, pair, n + 1))
                dve.tensor_tensor(hid[:, h, k, :], gated[:, n % 2, :], up_b[n % 2][:, :],
                                  ALU.mult).then_inc(f.hidden, 1)

            def ffn_residual(f, pair, h):
                dve.wait_ge(f.y, at(2, pair, h + 1))
                if f is f1:
                    dve.wait_ge(xr_in[h], at(16, pair, 16))
                    if later(pair, h, 2):
                        dve.wait_ge(xm_done, at(2, pair, h - 1))
                    dve.scalar_tensor_tensor(x1_c[:, h, :, :].rearrange("p t d -> p (t d)"), y_b[:, :], Y_SCALE,
                                             x_r[:, h, :, :].rearrange("p t d -> p (t d)"), ALU.mult, ALU.add
                                             ).then_inc(f.res, 1)
                else:
                    if later(pair, h, 2):
                        dve.wait_ge(stored[h], at(16, pair, 0))
                    for m in range(TPC):
                        x2 = xm[:, bass.ds(pair * HEADS_KV, HEADS_KV), h * TPC + m, :]
                        i = dve.scalar_tensor_tensor(
                            out_c[:, h, m, :].rearrange("p (j e) -> p j e", j=HEADS_KV),
                            y_b[:, P * m:P * m + P].rearrange("p (j e) -> p j e", j=HEADS_KV), Y_SCALE, x2,
                            ALU.mult, ALU.add)
                    i.then_inc(f.res, 1)

            def proj_moments(pair, h):
                dve.wait_ge(f1.res, at(2, pair, h + 1))
                if later(pair, h, 1):
                    dve.wait_ge(xn_ready, at(2, pair, h))
                moments(lambda m: x1_c[:, h, m, :], st6b, mvb[:, :, :], ln2, at(4, pair, 2 * h))

            def proj_residues(pair, h):
                dve.wait_ge(q1_done, at(2, pair, h + 1))
                dve.tensor_scalar(q_neg[:, :], q_b[:, :], 0.0, None, ALU.min).then_inc(q_min, 1)
                dve.tensor_tensor(q_r[:, :], q_b[:, :], q_p[:, h, 0, :], ALU.subtract).then_inc(q_res, 1)
                dve.wait_ge(k1_done, at(2, pair, h + 1))
                dve.tensor_tensor(k_r[:, :], k_b[0:KV, :], k_p[:, h, 0, :], ALU.subtract).then_inc(k_res, 1)

            def proj_thirds(pair, h):
                dve.wait_ge(q_expd, at(2, pair, h + 1))
                dve.scalar_tensor_tensor(q_elu[:, :], q_exp[:, :], -1.0, q_b[:, :], ALU.add, ALU.max
                                         ).then_inc(q_elud, 1)
                dve.wait_ge(q2_done, at(2, pair, h + 1))
                dve.tensor_tensor(q_p[:, h, 2, :], q_r[:, :], q_p[:, h, 1, :], ALU.subtract).then_inc(q3_done, 1)
                dve.wait_ge(k2_done, at(2, pair, h + 1))
                dve.tensor_tensor(k_p[:, h, 2, :], k_r[:, :], k_p[:, h, 1, :], ALU.subtract).then_inc(k3_done, 1)

            def memory_read(pair, h):
                dve.wait_ge(am_ps, at(2, pair, h + 1))
                dve.reciprocal(r_den[:, 0, :], k_b[:, 0:TPC * GROUP]).then_inc(am_step, 1)
                dve.wait_ge(am_step, at(4, pair, 2 * h + 1))
                dve.tensor_scalar(r_den[:, 1, :], r_den[:, 0, :], w_col, None, ALU.mult).then_inc(am_step, 1)
                dve.wait_ge(am_step, at(4, pair, 2 * h + 2))
                if isinstance(pair, int) and 2 * pair + h == CHUNKS - 1:
                    dve.wait_ge(xm_done, CHUNKS - 1)
                dve.tensor_tensor(a_mem[:, :, :].rearrange("p t (g e) -> p (t g) e", g=GROUP),
                                  q_b[:, :].rearrange("p (n e) -> p n e", e=KV),
                                  r_den[:, 1, :].unsqueeze(2).broadcast_to([P, TPC * GROUP, KV]),
                                  ALU.mult).then_inc(am_done, 1)

            dve.wait_ge(mw_exp, 1)
            dve.tensor_scalar(mix[:, 2:4], mix[:, 0:2], 1.0, None, ALU.add).then_inc(mix_step, 1)
            dve.wait_ge(mix_step, 1)
            dve.reciprocal(mix[:, 4:6], mix[:, 2:4]).then_inc(mix_step, 1)
            dve.wait_ge(mix_step, 2)
            dve.tensor_copy(omw_16[:, :, :].rearrange("p a b -> p (a b)"), omw_col.broadcast_to([P, 16])
                            ).then_inc(mix_step, 1)

            def phase1(pair, h):
                do(lambda *c: ffn_moments(f1, *c), pair, h, 2)
                do(lambda *c: ffn_hidden(f1, *c, 1), pair, h, 0)
                do(proj_thirds, pair, h, -2)
                do(lambda *c: ffn_hidden(f1, *c, 2), pair, h, 0)
                do(lambda *c: ffn_hidden(f1, *c, 0), pair, h, 1)
                do(memory_read, pair, h, -2)
                do(lambda *c: ffn_residual(f1, *c), pair, h, 0)
                do(proj_residues, pair, h, -1)
                do(proj_moments, pair, h, 0)

            def row_maxima(K, par, st):
                for q in range(2 * GROUP):
                    n = 4 * st + q
                    dve.wait_ge(a_ready, at(32, K, n + 1))
                    dve.tensor_reduce(mx[:, par, q // 2, st, q % 2:q % 2 + 1], a_b[n % 3][:, :], AX.X, ALU.max
                                      ).then_inc(a_used, 1)

            def whole_maxima(K, par):
                dve.wait_ge(a_used, at(32, K, 32))
                dve.tensor_reduce(m16[:, par, :, :], mx[:, par, :, :, :], AX.X, ALU.max).then_inc(m_max, 1)

            def reciprocals(J, par):
                dve.wait_ge(o_sb, at(1, J, 1))
                dve.reciprocal(r_sum[:, par, :, :], o_s[:, par, :, :, DH]).then_inc(o_rec, 1)

            chunk_loop(dve, phase1)
            for st in range(TILES // 2):
                row_maxima(0, 0, st)
            phase1(CHUNKS // 2, 0)
            for st in range(TILES // 2, TILES):
                row_maxima(0, 0, st)
            phase1(CHUNKS // 2, 1)
            whole_maxima(0, 0)
            for st in range(LEAD):
                row_maxima(1, 1, st)

            def pairs(it, first, last):
                for u in range(SLOTS):
                    J = it * SLOTS + u
                    for i in range(TILES):
                        n, st = ahead(i)
                        if not (last and u + n >= SLOTS):
                            row_maxima(J + n, (u + n) % 2, st)
                            if st == TILES - 1:
                                whole_maxima(J + n, (u + n) % 2)
                        if i == 3 and not (first and u == 0):
                            reciprocals(J - 1, (u - 1) % 2)

            def before_last():
                ffn_moments(f3, 0, 0)
                ffn_moments(f3, 0, 1)

            attention_loop(dve, pairs, before_last)
            ffn_hidden(f3, 0, 0, 0)
            reciprocals(PAIRS - 1, 1)

            def phase3(pair, h):
                do(lambda *c: ffn_moments(f3, *c), pair, h, 2)
                ffn_hidden(f3, pair, h, 1)
                ffn_hidden(f3, pair, h, 2)
                do(lambda *c: ffn_hidden(f3, *c, 0), pair, h, 1)
                ffn_residual(f3, pair, h)

            phase3_loop(dve, phase3)

        @block.tensor
        def _(pe):
            mm = pe.matmul

            def ffn_transpose(f, pair, h):
                pe.wait_ge(f.xhat, at(2, pair, h + 1))
                if f is f1 and later(pair, h, 3):
                    pe.wait_ge(v_sb, at(2, pair, h - 2))
                for m in range(TPC):
                    i = pe.transpose(tr_b[:, P * m:P * m + P], x_hat[:, h, m, :], ident[:, :])
                i.then_inc(f.xt_ps, 1)

            def ffn_up(f, pair, h, k):
                n = KH * h + k
                if k == 0:
                    pe.wait_ge(f.xt, at(2, pair, h + 1))
                if later(pair, h, 1) or k == 2:
                    pe.wait_ge(f.hidden, at(2 * KH, pair, n - 1))
                mm(gate_b[n % 2][:, :], w_f[:, 0, P * k:P * k + P], x_t[:, h, :], start=True, stop=True)
                mm(up_b[n % 2][:, :], w_f[:, 1, P * k:P * k + P], x_t[:, h, :], start=True, stop=True).then_inc(f.gu, 1)

            def ffn_down(f, pair, h):
                pe.wait_ge(f.hidden, at(2 * KH, pair, KH * h + KH))
                if later(pair, h, 1):
                    pe.wait_ge(f.res, at(2, pair, h))
                for m in range(TPC):
                    for k in range(KH):
                        i = mm(y_b[:, P * m:P * m + P], hid[:, h, k, P * m:P * m + P], w_f[:, 2, P * k:P * k + P],
                               start=(k == 0), stop=(k == KH - 1))
                i.then_inc(f.y, 1)

            def proj_transpose(pair, h):
                pe.wait_ge(xn_ready, at(2, pair, h + 1))
                for m in range(TPC):
                    i = pe.transpose(tr_b[:, P * m:P * m + P], xn_hat[:, m, :], ident[:, :])
                i.then_inc(xn_ps, 1)

            def proj(pair, h):
                pe.wait_ge(xn_sb, at(2, pair, h + 1))
                if later(pair, h, 1):
                    pe.wait_ge(am_done, at(2, pair, h))
                mm(q_b[:, :], wq_s[:, :], xn_t[:, :], start=True, stop=True).then_inc(q_ps, 1)
                mm(k_b[0:KV, :], wk_s[:, :], xn_t[:, :], start=True, stop=True).then_inc(k_ps, 1)
                for m in range(TPC):
                    i = mm(tr_b[:, KV * m:KV * m + KV], xn_t[:, P * m:P * m + P], wv_s[:, :], start=True, stop=True)
                i.then_inc(v_ps, 1)

            def memory_product(pair, h):
                pe.wait_ge(q_elud, at(2, pair, h + 1))
                pe.wait_ge(q3_done, at(2, pair, h + 1))
                pe.wait_ge(k_res, at(2, pair, h + 1))
                for m in range(TPC):
                    mm(q_b[:, P * m:P * m + P], q_elu[:, P * m:P * m + P], mem_s[:, :], start=True, stop=True)
                    i = mm(k_b[:, GROUP * m:GROUP * (m + 1)], q_elu[:, P * m:P * m + P], norm_s[:, :],
                           start=True, stop=True)
                i.then_inc(am_ps, 1)

            pe.wait_ge(ident_set, 3)
            pe.wait_ge(w_cast, 1)

            def phase1(pair, h):
                do(lambda *c: ffn_up(f1, *c, 1), pair, h, 0)
                do(lambda *c: ffn_transpose(f1, *c), pair, h, 1)
                do(lambda *c: ffn_up(f1, *c, 2), pair, h, 0)
                do(lambda *c: ffn_up(f1, *c, 0), pair, h, 1)
                if isinstance(pair, int) and pair == 0 and h == 1:
                    pe.wait_ge(mem_loaded, 16 * 7)
                do(memory_product, pair, h, -2)
                do(proj_transpose, pair, h, -1)
                do(lambda *c: ffn_down(f1, *c), pair, h, 0)
                do(proj, pair, h, -1)

            def max_scores(it, u, J, n, st, q):
                K, slot = J + n, (u + n) % SLOTS
                idx = 4 * st + q
                if idx == 0:
                    pe.wait_ge(loaded[slot], at(LOADS * 16, it + (u + n) // SLOTS, LOADS * 16))
                if not (isinstance(K, int) and K == 0 and idx < 3):
                    pe.wait_ge(a_used, at(32, K, (-1, 0, -2)[idx] if idx < 3 else idx - 2))
                g, half = q // 2, q % 2
                mm(a_b[idx % 3][:, :], q_op[0:MAXROW, slot, g, P * st:P * st + P],
                   k_op[0:MAXROW, slot, 512 * half:512 * half + 512], start=True, stop=True).then_inc(a_ready, 1)

            def scores(J, u, i, q):
                idx = 4 * i + q
                if idx == 0:
                    pe.wait_ge(m_in, at(16, J, 16))
                if not (isinstance(J, int) and J == 0 and idx < 3):
                    pe.wait_ge(p_ready, at(32, J, (-1, 0, -2)[idx] if idx < 3 else idx - 2))
                g, half = q // 2, q % 2
                mm(t_b[idx % 3][:, :], k_op[0:MAXROW + PARTS, u, P * i:P * i + P],
                   q_op[0:MAXROW + PARTS, u, g, 512 * half:512 * half + 512], start=True, stop=True
                   ).then_inc(t_ready, 1)

            def weigh_values(J, par, i):
                pe.wait_ge(p_ready, at(32, J, 4 * i + 4))
                if i == 0:
                    pe.wait_ge(v9_ready, at(1, J, 1))
                    if not (isinstance(J, int) and J == 0):
                        pe.wait_ge(pv_sb, at(1, J, 0))
                for q in range(2 * GROUP):
                    m = mm(pv_b[VPAD * q:VPAD * q + VPAD, :], v9[:, par, i, :], probs[:, i % 2, q, :],
                           start=(i == 0), stop=(i == TILES - 1))
                if i == TILES - 1:
                    m.then_inc(pv_done, 1)

            def transpose_max(K, par):
                if not (isinstance(K, int) and K < 2):
                    pe.wait_ge(o_sb, at(1, K, -1))
                wait_alone(pe, m_split, at(5, K, 5))
                pe.transpose(misc_b[:, :].bitcast(bf16)[0:MCOLS, 0:P],
                             m_parts[:, par, :, :, :].rearrange("p a g t -> p (a g t)"), ident_b[:, :]
                             ).then_inc(m_ps, 1)

            def transpose_sums(J, par):
                pe.wait_ge(pv_sb, at(1, J, 1))
                if not (isinstance(J, int) and J == PAIRS - 1):
                    pe.wait_ge(m_sb, at(1, J, 2))
                else:
                    pe.wait_ge(o_sb, PAIRS - 1)
                for c in range(4):
                    i = pe.transpose(misc_b[:, P * c:P * c + P], o_t[:, par, P * c:P * c + P], ident[:, :])
                i.then_inc(o_ps, 1)

            chunk_loop(pe, phase1)
            pe.wait_ge(f1.hidden, KH * CHUNKS)
            for st in range(TILES // 2):
                for q in range(2 * GROUP):
                    max_scores(0, 0, 0, 0, st, q)
            phase1(CHUNKS // 2, 0)
            for st in range(TILES // 2, TILES):
                for q in range(2 * GROUP):
                    max_scores(0, 0, 0, 0, st, q)
            phase1(CHUNKS // 2, 1)
            for st in range(LEAD):
                for q in range(2 * GROUP):
                    max_scores(0, 0, 0, 1, st, q)
            pe.wait_ge(am_done, CHUNKS)
            pe.wait_ge(v_sb, CHUNKS)
            transpose_max(0, 0)

            def pairs(it, first, last):
                for u in range(SLOTS):
                    J = it * SLOTS + u
                    for i in range(TILES):
                        n, st = ahead(i)
                        if i == 2 and not (first and u == 0):
                            transpose_sums(J - 1, (u - 1) % 2)
                        if i == 6 and not (last and u == SLOTS - 1):
                            transpose_max(J + 1, (u + 1) % 2)
                        for q in range(2 * GROUP):
                            scores(J, u, i, q)
                            if not (last and u + n >= SLOTS):
                                max_scores(it, u, J, n, st, q)
                        if i > 0:
                            weigh_values(J, u % 2, i - 1)
                        elif not (first and u == 0):
                            weigh_values(J - 1, (u - 1) % 2, TILES - 1)

            attention_loop(pe, pairs)
            pe.wait_ge(p_ready, 32 * PAIRS)
            ffn_transpose(f3, 0, 0)
            weigh_values(PAIRS - 1, 1, TILES - 1)
            ffn_up(f3, 0, 0, 0)
            transpose_sums(PAIRS - 1, 1)

            def phase3(pair, h):
                ffn_up(f3, pair, h, 1)
                do(lambda *c: ffn_transpose(f3, *c), pair, h, 1)
                ffn_up(f3, pair, h, 2)
                do(lambda *c: ffn_up(f3, *c, 0), pair, h, 1)
                ffn_down(f3, pair, h)

            phase3_loop(pe, phase3)


def kernel(L0_attn_x, L0_attn_Wq, L0_attn_Wk, L0_attn_Wv, L0_attn_memory, L0_attn_memory_norm,
           L0_attn_memory_weight, L0_ffn_w_gate, L0_ffn_w_up, L0_ffn_w_down):
    import numpy as np
    import concourse.bacc as bacc
    from concourse.bass_utils import run_bass_kernel_spmd

    arrays = {
        "x": L0_attn_x, "wq": L0_attn_Wq, "wk": L0_attn_Wk, "wv": L0_attn_Wv, "memory": L0_attn_memory,
        "memory_norm": L0_attn_memory_norm, "memory_weight": L0_attn_memory_weight,
        "wg_t": np.asarray(L0_ffn_w_gate).T, "wu_t": np.asarray(L0_ffn_w_up).T, "wd_t": np.asarray(L0_ffn_w_down).T,
    }
    arrays = {n: np.ascontiguousarray(a) for n, a in arrays.items()}
    nc = bacc.Bacc("TRN2", target_bir_lowering=False, num_devices=1)
    args = [nc.dram_tensor(n, a.shape, mybir.dt.from_np(a.dtype), kind="ExternalInput").ap()
            for n, a in arrays.items()]
    out = nc.dram_tensor("out", (B, S, D), mybir.dt.float32, kind="ExternalOutput").ap()
    build(nc, *args, out)
    run = run_bass_kernel_spmd(nc, [arrays], core_ids=[0])
    return run.results[0]["out"]
```

```python
from contextlib import ExitStack

import concourse.bass as bass
from concourse import mybir

P = 128
B, S, D = 4, 1024, 128
HEADS_KV, GROUP, DH = 8, 2, 8
KV = HEADS_KV * DH
HID = 384
KH = HID // P
CH = 512
TPC = CH // P
CHUNKS = B * S // CH
TILES = S // P
PAIRS = B * HEADS_KV
PARTS = 3
QROWS = PARTS * PARTS * DH
MAXROW = 96
ZROW = QROWS // 32 * 32
SLOTS = 4
LEAD = 3
LN_EPS = 1e-5
FFN_SCALE = 1.0 / 127.0
TANH_SCALE = 0.5 * FFN_SCALE
Y_SCALE = 0.5 * 0.5 * FFN_SCALE ** 3
SM_SCALE = float(DH) ** -0.5
VW = DH + 1
VPAD = 32
MCOLS = GROUP * PARTS * TILES


def build(nc, x, wq, wk, wv, memory, memory_norm, memory_weight, wg_t, wu_t, wd_t, out):
    f32, bf16, i32 = mybir.dt.float32, mybir.dt.bfloat16, mybir.dt.int32
    ALU, ACT, AX = mybir.AluOpType, mybir.ActivationFunctionType, mybir.AxisListType

    q_spill = nc.dram_tensor("q_spill", [PAIRS * GROUP * DH, PARTS, S], bf16, kind="Internal").ap()
    k_spill = nc.dram_tensor("k_spill", [PAIRS * DH, PARTS, S], bf16, kind="Internal").ap()
    x_rows = x.rearrange("b (t p) d -> p (b t) d", p=P)
    out_rows = out.rearrange("b (t p) d -> p (b t) d", p=P)

    ctx = ExitStack()
    with ctx:
        def sb(name, shape, dt=f32):
            return ctx.enter_context(nc.sbuf_tensor(name, shape, dt))

        def bank(name):
            return ctx.enter_context(nc.psum_tensor(name, [P, 512], f32))

        def sem(name):
            return ctx.enter_context(nc.semaphore(name))

        ident = sb("ident", [P, P])
        ident_b = sb("ident_b", [P, P], bf16)
        wq_s, wk_s, wv_s = sb("wq_s", [P, D]), sb("wk_s", [P, KV]), sb("wv_s", [P, KV])
        mem_s = sb("mem_s", [P, D])
        norm_s = sb("norm_s", [P, GROUP])
        w_int = sb("w_int", [P, 3, HID], i32)
        w_f = sb("w_f", [P, 3, HID])
        mw = sb("mw", [P, 1])
        mix = sb("mix", [P, 6])
        w_col, omw_col = mix[:, 4:5], mix[:, 5:6]
        x_n = sb("x_n", [P, 2, TPC, D])
        x_r = sb("x_r", [P, 2, TPC, D])
        st6 = sb("st6", [P, 2, TPC, 6])
        mv = sb("mv", [P, 2, TPC, 2])
        rstd = sb("rstd", [P, 2, 4, TPC])
        neg_half, neg_one = sb("neg_half", [P, TPC]), sb("neg_one", [P, TPC])
        x_hat = sb("x_hat", [P, 2, TPC, D])
        x_t = sb("x_t", [P, 2, CH])
        th = sb("th", [P, 2, CH])
        gated = sb("gated", [P, 2, CH])
        hid = sb("hid", [P, 2, KH, CH])
        out_c = sb("out_c", [P, 2, TPC, D])
        x1_c = sb("x1_c", [P, 2, TPC, D])
        st6b = sb("st6b", [P, TPC, 6])
        mvb = sb("mvb", [P, TPC, 2])
        rstdb = sb("rstdb", [P, 4, TPC])
        xn_hat = sb("xn_hat", [P, TPC, D])
        xn_t = sb("xn_t", [P, CH])
        q_p = sb("q_p", [P, 2, PARTS, CH], bf16)
        k_p = sb("k_p", [KV, 2, PARTS, CH], bf16)
        q_r, k_r = sb("q_r", [P, CH]), sb("k_r", [KV, CH])
        q_neg, q_exp, q_elu = sb("q_neg", [P, CH]), sb("q_exp", [P, CH]), sb("q_elu", [P, CH])
        r_den = sb("r_den", [P, 2, TPC * GROUP])
        a_mem = sb("a_mem", [P, TPC, D])
        v_all = sb("v_all", [P, PAIRS, TILES * VW])
        xm = sb("xm", [P, PAIRS, TILES, GROUP * DH])
        q_op = sb("q_op", [P, SLOTS, GROUP, S], bf16)
        k_op = sb("k_op", [P, SLOTS, S], bf16)
        mx = sb("mx", [P, 2, GROUP, TILES, 2])
        m16 = sb("m16", [P, 2, GROUP, TILES])
        m_neg, m_res = sb("m_neg", [P, GROUP, TILES]), sb("m_res", [P, GROUP, TILES])
        m_parts = sb("m_parts", [P, 2, PARTS, GROUP, TILES], bf16)
        m_rows = sb("m_rows", [MCOLS, 2, P], bf16)
        probs = sb("probs", [P, 2, 2 * GROUP, 512])
        v9 = sb("v9", [P, 2, TILES, VPAD])
        o_t = sb("o_t", [P, 2, 512])
        o_s = sb("o_s", [P, 2, 4, 4, VW])
        r_sum = sb("r_sum", [P, 2, 4, 4])
        r_mix = sb("r_mix", [P, 4, 4])
        omw_16 = sb("omw_16", [P, 4, 4])
        o_n = sb("o_n", [P, 4, 4, DH])

        banks = [bank(f"bank{n}") for n in range(8)]
        gate_b, up_b = (banks[0], banks[2]), (banks[1], banks[3])
        tr_b, y_b, q_b, k_b = banks[4], banks[5], banks[6], banks[7]
        a_b, t_b, pv_b, misc_b = banks[0:3], banks[3:6], banks[6], banks[7]

        xn_in, xr_in = [sem("xn_in0"), sem("xn_in1")], [sem("xr_in0"), sem("xr_in1")]
        w_loaded = sem("w_loaded")
        mem_loaded, mw_loaded = sem("mem_loaded"), sem("mw_loaded")
        zeroed, ones_set, ident_set, op_set = sem("zeroed"), sem("ones_set"), sem("ident_set"), sem("op_set")
        w_cast, mw_exp, mix_step = sem("w_cast"), sem("mw_exp"), sem("mix_step")

        class FfnSems:
            def __init__(self, tag):
                self.src, self.ln, self.root, self.xhat = (sem(f"{tag}_{n}") for n in ("src", "ln", "root", "xhat"))
                self.scale = sem(f"{tag}_scale")
                self.xt_ps, self.xt, self.gu, self.th = (sem(f"{tag}_{n}") for n in ("xt_ps", "xt", "gu", "th"))
                self.gated, self.hidden, self.y, self.res = (
                    sem(f"{tag}_{n}") for n in ("gated", "hidden", "y", "res"))

        f1, f3 = FfnSems("ffn1"), FfnSems("ffn2")
        ln2, root2, scale2 = sem("ln2"), sem("root2"), sem("scale2")
        xn_ready, xn_ps, xn_sb = sem("xn_ready"), sem("xn_ps"), sem("xn_sb")
        q_ps, k_ps, v_ps, v_sb = sem("q_ps"), sem("k_ps"), sem("v_ps"), sem("v_sb")
        q1_done, q_res, q2_done, q3_done = sem("q1_done"), sem("q_res"), sem("q2_done"), sem("q3_done")
        k1_done, k_res, k2_done, k3_done = sem("k1_done"), sem("k_res"), sem("k2_done"), sem("k3_done")
        q_min, q_expd, q_elud, am_ps = sem("q_min"), sem("q_expd"), sem("q_elud"), sem("am_ps")
        am_step, am_done, xm_done = sem("am_step"), sem("am_done"), sem("xm_done")
        spilled = [sem("spilled0"), sem("spilled1")]
        loaded = [sem(f"loaded{s}") for s in range(SLOTS)]
        a_ready, a_used, m_max, m_split, m_ps, m_sb, m_in = (
            sem(n) for n in ("a_ready", "a_used", "m_max", "m_split", "m_ps", "m_sb", "m_in"))
        t_ready, p_ready, pv_done, pv_sb = (sem(n) for n in ("t_ready", "p_ready", "pv_done", "pv_sb"))
        v9_ready, o_ps, o_sb, o_rec, o_norm, xm_added = (
            sem(n) for n in ("v9_ready", "o_ps", "o_sb", "o_rec", "o_norm", "xm_added"))
        stored = [sem("stored0"), sem("stored1")]
        waits_passed = sem("waits_passed")
        CREDIT = 16
        AHEAD_CHUNK = {0: (0, 0), 1: (0, 1), 3: (1, 0)}
        LOADS = GROUP + PARTS
        block = ctx.enter_context(nc.Block())

        def at(n, c, k):
            return c * n + k

        def chunk(pair, h, k):
            d, h = divmod(h + k, 2)
            there = not isinstance(pair, int) or 0 <= 2 * (pair + d) + h < CHUNKS
            return (pair + d, h) if there else None

        def do(step, pair, h, k, *more):
            c = chunk(pair, h, k)
            if c is not None:
                step(*c, *more)

        def later(pair, h, n):
            return not isinstance(pair, int) or 2 * pair + h >= n

        def chunk_loop(eng, body):
            for pair in (-1, 0):
                body(pair, 0)
                body(pair, 1)
            with eng.Fori(1, CHUNKS // 2 - 1) as pair:
                body(pair, 0)
                body(pair, 1)
            body(CHUNKS // 2 - 1, 0)
            body(CHUNKS // 2 - 1, 1)

        def phase3_loop(eng, body):
            body(0, 0)
            body(0, 1)
            with eng.Fori(1, CHUNKS // 2 - 1) as pair:
                body(pair, 0)
                body(pair, 1)
            body(CHUNKS // 2 - 1, 0)
            body(CHUNKS // 2 - 1, 1)

        def attention_loop(eng, body, before_last=None):
            body(0, True, False)
            with eng.Fori(1, PAIRS // SLOTS - 1) as it:
                body(it, False, False)
            if before_last:
                before_last()
            body(PAIRS // SLOTS - 1, False, True)

        def wait_alone(eng, semaphore, count):
            eng.wait_ge(semaphore, count)
            if not isinstance(count, int):
                eng.sem_inc(waits_passed, 1)

        def ahead(i):
            return (1, i + LEAD) if i + LEAD < TILES else (2, i + LEAD - TILES)

        @block.sync
        def _(sp):
            def rows_of(pair, h):
                return x_rows[:, bass.ds(pair * (2 * TPC) + h * TPC, TPC), :]

            def load_n(pair, h):
                if later(pair, h, 2):
                    sp.wait_ge(f1.xhat, at(2, pair, h - 1))
                sp.dma_start(x_n[:, h, :, :], rows_of(pair, h)).then_inc(xn_in[h], 16)

            def load_r(pair, h):
                if later(pair, h, 2):
                    sp.wait_ge(f1.res, at(2, pair, h - 1))
                sp.dma_start(x_r[:, h, :, :], rows_of(pair, h)).then_inc(xr_in[h], 16)

            def load_pair(J, slot):
                R = DH * PARTS
                for g in range(GROUP):
                    v = q_spill[bass.ds(J * (GROUP * DH) + g * DH, DH), :, :]
                    sp.dma_start(q_op[0:QROWS, slot, g, :],
                                 bass.AP(v.tensor, v.offset, [[0, PARTS], [S, R], [1, S]])).then_inc(loaded[slot], 16)
                for a in range(PARTS):
                    v = k_spill[bass.ds(J * DH, DH), a, :]
                    sp.dma_start(k_op[R * a:R * a + R, slot, :],
                                 bass.AP(v.tensor, v.offset, [[PARTS * S, DH], [0, PARTS], [1, S]])
                                 ).then_inc(loaded[slot], 16)

            def spill(pair, h):
                sp.wait_ge(q3_done, at(2, pair, h + 1))
                sp.dma_start(q_spill[bass.ds(pair * P, P), :, h * CH:(h + 1) * CH],
                             q_p[:, h, :, :]).then_inc(spilled[h], 16)
                sp.wait_ge(k3_done, at(2, pair, h + 1))
                sp.dma_start(k_spill[bass.ds(pair * KV, KV), :, h * CH:(h + 1) * CH],
                             k_p[:, h, :, :]).then_inc(spilled[h], 16)

            def phase1(pair, h):
                do(load_n, pair, h, 3)
                do(load_r, pair, h, 1)
                do(spill, pair, h, -2)

            load_n(0, 0)
            load_n(0, 1)
            sp.dma_start(mw[:, :], bass.AP(memory_weight.tensor, memory_weight.offset, [[0, P], [1, 1]])
                         ).then_inc(mw_loaded, 16)
            load_r(0, 0)
            sp.dma_start(wq_s[:, :], wq).then_inc(mem_loaded, 16)
            sp.dma_start(wk_s[:, :], wk).then_inc(mem_loaded, 16)
            sp.dma_start(wv_s[:, :], wv).then_inc(mem_loaded, 16)
            sp.wait_ge(zeroed, 1)
            for g in range(GROUP):
                sp.dma_start(mem_s[KV * g:KV * g + KV, KV * g:KV * g + KV], memory).then_inc(mem_loaded, 16)
                sp.dma_start(norm_s[KV * g:KV * g + KV, g:g + 1],
                             memory_norm.rearrange("(n a) -> n a", a=1)).then_inc(mem_loaded, 16)
            load_n(1, 0)
            phase1(0, 0)
            phase1(0, 1)
            with sp.Fori(1, CHUNKS // 2 - 2) as pair:
                phase1(pair, 0)
                phase1(pair, 1)
            for c in range(CHUNKS - 4, CHUNKS):
                if c == CHUNKS - 2:
                    sp.wait_ge(op_set, 3)
                    for h in range(2):
                        sp.wait_ge(spilled[h], CREDIT + 32)
                    load_pair(0, 0)
                phase1(*divmod(c, 2))
            for s in range(1, SLOTS - 1):
                load_pair(s, s)
            spill(CHUNKS // 2 - 1, 0)
            spill(CHUNKS // 2 - 1, 1)

            def m_to_operand(K, slot, par):
                sp.wait_ge(m_sb, at(1, K, 1))
                sp.dma_start(q_op[MAXROW:MAXROW + PARTS, slot, :, :].rearrange("a g (t p) -> a (g t) p", p=P),
                             m_rows[:, par, :]).then_inc(m_in, 16)

            m_to_operand(0, 0, 0)
            for h in range(2):
                sp.wait_ge(spilled[h], CREDIT + 32 * B)

            def pairs(it, first, last):
                for u in range(SLOTS):
                    J = it * SLOTS + u
                    if not (last and u > 0):
                        if not (first and u == 0):
                            sp.wait_ge(t_ready, at(32, J, 0))
                        load_pair(J + SLOTS - 1, (u + SLOTS - 1) % SLOTS)
                    if not (last and u == SLOTS - 1):
                        m_to_operand(J + 1, (u + 1) % SLOTS, (u + 1) % 2)

            attention_loop(sp, pairs)

            def store(pair, h):
                sp.wait_ge(f3.res, at(2, pair, h + 1))
                sp.dma_start(out_rows[:, bass.ds(pair * (2 * TPC) + h * TPC, TPC), :],
                             out_c[:, h, :, :]).then_inc(stored[h], 16)

            with sp.Fori(0, CHUNKS // 2) as pair:
                store(pair, 0)
                store(pair, 1)
            for h in range(2):
                sp.wait_ge(stored[h], 16 * (CHUNKS // 2))

        @block.gpsimd
        def _(pool):
            def constant_rows():
                pool.memset(q_op[:, :, :, :], 0.0).then_inc(op_set, 1)
                pool.wait_ge(op_set, 2)
                pool.memset(k_op[MAXROW:P, :, :], 1.0).then_inc(op_set, 1)
                pool.wait_ge(op_set, 3)

            for h in range(2):
                pool.sem_inc(spilled[h], CREDIT)
            pool.memset(neg_half[:, :], -0.5)
            pool.memset(neg_one[:, :], -1.0)
            pool.memset(mem_s[:, :], 0.0)
            pool.memset(norm_s[:, :], 0.0).then_inc(zeroed, 1)
            pool.memset(ident[:, :], 0.0)
            pool.memset(ident_b[:, :], 0.0).then_inc(ident_set, 1)
            pool.wait_ge(ident_set, 1)
            for m in (ident, ident_b):
                pool.affine_select(out=m[:, :], in_=m[:, :], compare_op=ALU.not_equal, fill=1.0, base=0,
                                   pattern=[[-1, P]], channel_multiplier=1).then_inc(ident_set, 1)

            def x1_plus_memory(pair, h):
                wait_alone(pool, am_done, at(2, pair, h + 1))
                dst = xm[:, bass.ds(pair * HEADS_KV, HEADS_KV), h * TPC:(h + 1) * TPC, :]
                for m in range(TPC):
                    i = pool.tensor_tensor(
                        dst[:, :, m, :], a_mem[:, m, :].rearrange("p (j e) -> p j e", j=HEADS_KV),
                        x1_c[:, h, m, :].rearrange("p (j e) -> p j e", j=HEADS_KV), ALU.add)
                i.then_inc(xm_done, 1)

            def scale_and_bias(agg, rs, steps, n, ready):
                pool.tensor_scalar(rs[:, 0, :], agg[:, :, 1], LN_EPS, None, ALU.add)
                pool.tensor_tensor(rs[:, 2, :], agg[:, :, 0], neg_one[:, :], ALU.mult).then_inc(steps, 1)
                wait_alone(pool, steps, n + 1)
                pool.tensor_tensor(rs[:, 1, :], rs[:, 0, :], neg_half[:, :], ALU.pow).then_inc(steps, 1)
                wait_alone(pool, steps, n + 2)
                pool.tensor_tensor(rs[:, 3, :], rs[:, 2, :], rs[:, 1, :], ALU.mult).then_inc(ready, 1)

            def ffn_scale(f, pair, h):
                wait_alone(pool, f.ln, at(4, pair, 2 * h + 2))
                scale_and_bias(mv[:, h, :, :], rstd[:, h, :, :], f.root, at(4, pair, 2 * h), f.scale)

            def ffn1_scale(pair, h):
                ffn_scale(f1, pair, h)

            def proj_scale(pair, h):
                wait_alone(pool, ln2, at(4, pair, 2 * h + 2))
                scale_and_bias(mvb, rstdb, root2, at(4, pair, 2 * h), scale2)

            def phase1(pair, h):
                do(proj_scale, pair, h, -1)
                do(x1_plus_memory, pair, h, -2)
                do(ffn1_scale, pair, h, 2)
                if isinstance(pair, int) and 2 * pair + h == -1:
                    constant_rows()

            pool.memset(v_all[:, :, :], 1.0).then_inc(ones_set, 1)
            chunk_loop(pool, phase1)
            pool.memset(v9[:, :, :, :], 0.0)
            phase1(CHUNKS // 2, 0)
            phase1(CHUNKS // 2, 1)

            def split_max(K, par):
                wait_alone(pool, m_max, at(1, K, 1))
                pool.tensor_scalar(m_neg[:, :, :], m16[:, par, :, :], -1.0, None, ALU.mult).then_inc(m_split, 1)
                wait_alone(pool, m_split, at(5, K, 1))
                pool.tensor_copy(m_parts[:, par, 0, :, :], m_neg[:, :, :]).then_inc(m_split, 1)
                wait_alone(pool, m_split, at(5, K, 2))
                pool.tensor_tensor(m_res[:, :, :], m_neg[:, :, :], m_parts[:, par, 0, :, :],
                                   ALU.subtract).then_inc(m_split, 1)
                wait_alone(pool, m_split, at(5, K, 3))
                pool.tensor_copy(m_parts[:, par, 1, :, :], m_res[:, :, :]).then_inc(m_split, 1)
                wait_alone(pool, m_split, at(5, K, 4))
                pool.tensor_tensor(m_parts[:, par, 2, :, :], m_res[:, :, :], m_parts[:, par, 1, :, :],
                                   ALU.subtract).then_inc(m_split, 1)

            def values(J, par):
                pool.tensor_copy(v9[:, par, :, 0:VW], v_all[:, J, :].rearrange("p (t e) -> p t e", t=TILES)
                                 if isinstance(J, int) else
                                 v_all[:, bass.ds(J, 1), :].rearrange("p a (t e) -> p (a t) e", t=TILES)
                                 ).then_inc(v9_ready, 1)

            def add_attention(J, par):
                wait_alone(pool, o_rec, at(1, J, 1))
                pool.tensor_tensor(r_mix[:, :, :], r_sum[:, par, :, :], omw_16[:, :, :], ALU.mult).then_inc(o_norm, 1)
                wait_alone(pool, o_norm, at(2, J, 1))
                pool.tensor_tensor(o_n[:, :, :, :], o_s[:, par, :, :, 0:DH],
                                   r_mix[:, :, :].unsqueeze(3).broadcast_to([P, 4, 4, DH]), ALU.mult
                                   ).then_inc(o_norm, 1)
                wait_alone(pool, o_norm, at(2, J, 2))
                for g in range(GROUP):
                    dst = xm[:, bass.ds(J, 1), :, DH * g:DH * g + DH].rearrange("p a (h c) d -> p (a h) c d", h=2)
                    i = pool.tensor_tensor(dst, dst, o_n[:, :, 2 * g:2 * g + 2, :].rearrange("p c h d -> p h c d"),
                                           ALU.add)
                i.then_inc(xm_added, 1)

            wait_alone(pool, v_sb, CHUNKS)
            values(0, 0)
            split_max(0, 0)

            def pairs(it, first, last):
                for u in range(SLOTS):
                    J = it * SLOTS + u
                    if not (last and u == SLOTS - 1):
                        if not (first and u == 0):
                            wait_alone(pool, pv_done, at(1, J, 0))
                        values(J + 1, (u + 1) % 2)
                    if last and u == SLOTS - 1:
                        gather_x2(1, 0)
                    if not (first and u == 0):
                        add_attention(J - 1, (u - 1) % 2)
                    if not (last and u == SLOTS - 1):
                        split_max(J + 1, (u + 1) % 2)
                    if last and u in AHEAD_CHUNK:
                        ffn_scale(f3, *AHEAD_CHUNK[u])

            def before_last():
                gather_x2(0, 0)
                gather_x2(0, 1)

            def gather_x2(pair, h):
                if later(pair, h, 2):
                    wait_alone(pool, f3.xhat, at(2, pair, h - 1))
                wait_alone(pool, xm_added, at(HEADS_KV, pair, HEADS_KV))
                src = xm[:, bass.ds(pair * HEADS_KV, HEADS_KV), h * TPC:(h + 1) * TPC, :]
                for m in range(TPC):
                    i = pool.tensor_copy(x_n[:, h, m, :].rearrange("p (j e) -> p j e", j=HEADS_KV), src[:, :, m, :])
                i.then_inc(f3.src, 1)

            attention_loop(pool, pairs, before_last)
            gather_x2(1, 1)
            add_attention(PAIRS - 1, 1)
            ffn_scale(f3, 1, 1)
            with pool.Fori(2, CHUNKS // 2) as pair:
                for h in range(2):
                    gather_x2(pair, h)
                    ffn_scale(f3, pair, h)

        @block.scalar
        def _(act):
            for n, w in enumerate((wg_t, wu_t)):
                act.dma_start(w_int[:, n, :], w).then_inc(w_loaded, 16)
            act.dma_start(w_int[:, 2, :].rearrange("p (k d) -> p k d", k=KH),
                          wd_t.rearrange("(k p) d -> p k d", p=P)).then_inc(w_loaded, 16)

            def normalise(src, dst, rs, ready, tiles=range(TPC)):
                for m in tiles:
                    i = act.activation(dst[:, m, :], src[:, m, :], ACT.Identity, bias=rs[:, 3, m:m + 1],
                                       scale=rs[:, 1, m:m + 1])
                if tiles[-1] == TPC - 1:
                    i.then_inc(ready, 1)

            def ffn_normalise(f, pair, h, tiles=range(TPC)):
                act.wait_ge(f.scale, at(2, pair, h + 1))
                if later(pair, h, 2):
                    act.wait_ge(f.xt_ps, at(2, pair, h - 1))
                normalise(x_n[:, h, :, :], x_hat[:, h, :, :], rstd[:, h, :, :], f.xhat, tiles)

            def proj_normalise(pair, h):
                act.wait_ge(scale2, at(2, pair, h + 1))
                if later(pair, h, 1):
                    act.wait_ge(xn_ps, at(2, pair, h))
                normalise(x1_c[:, h, :, :], xn_hat, rstdb, xn_ready)

            def ffn_xt(f, pair, h, src=tr_b):
                act.wait_ge(f.xt_ps, at(2, pair, h + 1))
                act.activation(x_t[:, h, :], src[:, :], ACT.Copy).then_inc(f.xt, 1)

            def ffn_tanh(f, pair, h, k):
                n = KH * h + k
                act.wait_ge(f.gu, at(2 * KH, pair, n + 1))
                if later(pair, h, 1) or k == 2:
                    act.wait_ge(f.hidden, at(2 * KH, pair, n - 1))
                act.activation(th[:, n % 2, :], gate_b[n % 2][:, :], ACT.Tanh, scale=TANH_SCALE).then_inc(f.th, 1)

            def proj_xn(pair, h):
                act.wait_ge(xn_ps, at(2, pair, h + 1))
                act.activation(xn_t[:, :], tr_b[:, :], ACT.Copy).then_inc(xn_sb, 1)

            def proj_first(pair, h):
                act.wait_ge(spilled[h], at(32, pair, CREDIT))
                act.wait_ge(q_ps, at(2, pair, h + 1))
                act.activation(q_p[:, h, 0, :], q_b[:, :], ACT.Copy).then_inc(q1_done, 1)
                act.wait_ge(k_ps, at(2, pair, h + 1))
                act.activation(k_p[:, h, 0, :], k_b[0:KV, :], ACT.Copy).then_inc(k1_done, 1)
                act.wait_ge(v_ps, at(2, pair, h + 1))
                if isinstance(pair, int) and pair == 0 and h == 0:
                    act.wait_ge(ones_set, 1)
                for m in range(TPC):
                    o = (h * TPC + m) * VW
                    i = act.activation(v_all[:, bass.ds(pair * HEADS_KV, HEADS_KV), o:o + DH],
                                       tr_b[:, KV * m:KV * m + KV].rearrange("p (j d) -> p j d", d=DH), ACT.Copy)
                i.then_inc(v_sb, 1)

            def proj_second(pair, h):
                act.wait_ge(q_min, at(2, pair, h + 1))
                act.activation(q_exp[:, :], q_neg[:, :], ACT.Exp).then_inc(q_expd, 1)
                act.wait_ge(q_res, at(2, pair, h + 1))
                act.activation(q_p[:, h, 1, :], q_r[:, :], ACT.Copy).then_inc(q2_done, 1)
                act.wait_ge(k_res, at(2, pair, h + 1))
                act.activation(k_p[:, h, 1, :], k_r[:, :], ACT.Copy).then_inc(k2_done, 1)

            def phase1(pair, h):
                if isinstance(pair, int) and 2 * pair + h == 0:
                    act.wait_ge(mw_loaded, 16)
                    act.activation(mix[:, 0:1], mw[:, :], ACT.Exp, scale=-1.0)
                    act.activation(mix[:, 1:2], mw[:, :], ACT.Exp).then_inc(mw_exp, 1)
                do(lambda *c: ffn_tanh(f1, *c, 1), pair, h, 0)
                do(lambda *c: ffn_xt(f1, *c), pair, h, 1)
                do(lambda *c: ffn_tanh(f1, *c, 2), pair, h, 0)
                do(proj_normalise, pair, h, -1)
                do(lambda *c: ffn_tanh(f1, *c, 0), pair, h, 1)
                do(proj_xn, pair, h, -1)
                do(proj_first, pair, h, -1)
                do(proj_second, pair, h, -1)
                do(lambda *c: ffn_normalise(f1, *c), pair, h, 2)

            chunk_loop(act, phase1)
            phase1(CHUNKS // 2, 0)

            def max_rows(K, par):
                act.wait_ge(m_ps, at(1, K, 1))
                act.activation(m_rows[:, par, :], misc_b[:, :].bitcast(bf16)[0:MCOLS, 0:P], ACT.Copy
                               ).then_inc(m_sb, 1)

            def sums_out(J, par):
                act.wait_ge(o_ps, at(1, J, 1))
                act.activation(o_s[:, par, :, :, :],
                               misc_b[:, :].rearrange("p (c q e) -> p c q e", c=4, q=4)[:, :, :, 0:VW],
                               ACT.Copy).then_inc(o_sb, 1)

            def pv_out(J, par):
                act.wait_ge(pv_done, at(1, J, 1))
                act.activation(o_t[:, par, :], pv_b[:, :], ACT.Copy).then_inc(pv_sb, 1)

            max_rows(0, 0)

            def pairs(it, first, last):
                for u in range(SLOTS):
                    J = it * SLOTS + u
                    for i in range(TILES):
                        for q in range(2 * GROUP):
                            act.wait_ge(t_ready, at(32, J, 4 * i + q + 1))
                            act.activation(probs[:, i % 2, q, :], t_b[(4 * i + q) % 3][:, :], ACT.Exp,
                                           scale=SM_SCALE).then_inc(p_ready, 1)
                            if i == 2 and q == 1 and not (first and u == 0):
                                sums_out(J - 1, (u - 1) % 2)
                            if i == 6 and q == 1 and not (last and u == SLOTS - 1):
                                max_rows(J + 1, (u + 1) % 2)
                        if i == 0 and not (first and u == 0):
                            pv_out(J - 1, (u - 1) % 2)
                        if last and u in (1, 2) and i < TPC:
                            ffn_normalise(f3, 0, u - 1, range(i, i + 1))
                        if last and u == 2 and i == 5:
                            ffn_xt(f3, 0, 0, banks[2])
                        if last and u == 2 and i == 7:
                            ffn_tanh(f3, 0, 0, 0)

            attention_loop(act, pairs)
            pv_out(PAIRS - 1, 1)

            def phase3(pair, h):
                ffn_tanh(f3, pair, h, 1)
                if isinstance(pair, int) and 2 * pair + h == 0:
                    sums_out(PAIRS - 1, 1)
                do(lambda *c: ffn_xt(f3, *c), pair, h, 1)
                ffn_tanh(f3, pair, h, 2)
                do(lambda *c: ffn_tanh(f3, *c, 0), pair, h, 1)
                do(lambda *c: ffn_normalise(f3, *c), pair, h, 2)

            phase3_loop(act, phase3)

        @block.vector
        def _(dve):
            def moments(src, s6, agg, steps, n):
                for m in range(TPC):
                    i = dve.bn_stats(s6[:, m, :], src(m))
                i.then_inc(steps, 1)
                wait_alone(dve, steps, n + 1)
                for m in range(TPC):
                    i = dve.bn_aggr(agg[:, m, :], s6[:, m, :])
                i.then_inc(steps, 1)

            def ffn_moments(f, pair, h):
                if later(pair, h, 2):
                    dve.wait_ge(f.xhat, at(2, pair, h - 1))
                if f is f1:
                    dve.wait_ge(xn_in[h], at(16, pair, 16))
                else:
                    dve.wait_ge(f.src, at(2, pair, h + 1))
                moments(lambda m: x_n[:, h, m, :], st6[:, h, :, :], mv[:, h, :, :], f.ln, at(4, pair, 2 * h))

            def ffn_hidden(f, pair, h, k):
                n = KH * h + k
                dve.wait_ge(f.th, at(2 * KH, pair, n + 1))
                dve.scalar_tensor_tensor(gated[:, n % 2, :], th[:, n % 2, :], 1.0, gate_b[n % 2][:, :],
                                         ALU.add, ALU.mult).then_inc(f.gated, 1)
                dve.wait_ge(f.gated, at(2 * KH, pair, n + 1))
                dve.tensor_tensor(hid[:, h, k, :], gated[:, n % 2, :], up_b[n % 2][:, :],
                                  ALU.mult).then_inc(f.hidden, 1)

            def ffn_residual(f, pair, h):
                dve.wait_ge(f.y, at(2, pair, h + 1))
                if f is f1:
                    dve.wait_ge(xr_in[h], at(16, pair, 16))
                    if later(pair, h, 2):
                        dve.wait_ge(xm_done, at(2, pair, h - 1))
                    dve.scalar_tensor_tensor(x1_c[:, h, :, :].rearrange("p t d -> p (t d)"), y_b[:, :], Y_SCALE,
                                             x_r[:, h, :, :].rearrange("p t d -> p (t d)"), ALU.mult, ALU.add
                                             ).then_inc(f.res, 1)
                else:
                    if later(pair, h, 2):
                        dve.wait_ge(stored[h], at(16, pair, 0))
                    for m in range(TPC):
                        x2 = xm[:, bass.ds(pair * HEADS_KV, HEADS_KV), h * TPC + m, :]
                        i = dve.scalar_tensor_tensor(
                            out_c[:, h, m, :].rearrange("p (j e) -> p j e", j=HEADS_KV),
                            y_b[:, P * m:P * m + P].rearrange("p (j e) -> p j e", j=HEADS_KV), Y_SCALE, x2,
                            ALU.mult, ALU.add)
                    i.then_inc(f.res, 1)

            def proj_moments(pair, h):
                dve.wait_ge(f1.res, at(2, pair, h + 1))
                if later(pair, h, 1):
                    dve.wait_ge(xn_ready, at(2, pair, h))
                moments(lambda m: x1_c[:, h, m, :], st6b, mvb[:, :, :], ln2, at(4, pair, 2 * h))

            def proj_residues(pair, h):
                dve.wait_ge(q1_done, at(2, pair, h + 1))
                dve.tensor_scalar(q_neg[:, :], q_b[:, :], 0.0, None, ALU.min).then_inc(q_min, 1)
                dve.tensor_tensor(q_r[:, :], q_b[:, :], q_p[:, h, 0, :], ALU.subtract).then_inc(q_res, 1)
                dve.wait_ge(k1_done, at(2, pair, h + 1))
                dve.tensor_tensor(k_r[:, :], k_b[0:KV, :], k_p[:, h, 0, :], ALU.subtract).then_inc(k_res, 1)

            def proj_thirds(pair, h):
                dve.wait_ge(q_expd, at(2, pair, h + 1))
                dve.scalar_tensor_tensor(q_elu[:, :], q_exp[:, :], -1.0, q_b[:, :], ALU.add, ALU.max
                                         ).then_inc(q_elud, 1)
                dve.wait_ge(q2_done, at(2, pair, h + 1))
                dve.tensor_tensor(q_p[:, h, 2, :], q_r[:, :], q_p[:, h, 1, :], ALU.subtract).then_inc(q3_done, 1)
                dve.wait_ge(k2_done, at(2, pair, h + 1))
                dve.tensor_tensor(k_p[:, h, 2, :], k_r[:, :], k_p[:, h, 1, :], ALU.subtract).then_inc(k3_done, 1)

            def memory_read(pair, h):
                dve.wait_ge(am_ps, at(2, pair, h + 1))
                dve.reciprocal(r_den[:, 0, :], k_b[:, 0:TPC * GROUP]).then_inc(am_step, 1)
                dve.wait_ge(am_step, at(4, pair, 2 * h + 1))
                dve.tensor_scalar(r_den[:, 1, :], r_den[:, 0, :], w_col, None, ALU.mult).then_inc(am_step, 1)
                dve.wait_ge(am_step, at(4, pair, 2 * h + 2))
                if isinstance(pair, int) and 2 * pair + h == CHUNKS - 1:
                    dve.wait_ge(xm_done, CHUNKS - 1)
                dve.tensor_tensor(a_mem[:, :, :].rearrange("p t (g e) -> p (t g) e", g=GROUP),
                                  q_b[:, :].rearrange("p (n e) -> p n e", e=KV),
                                  r_den[:, 1, :].unsqueeze(2).broadcast_to([P, TPC * GROUP, KV]),
                                  ALU.mult).then_inc(am_done, 1)

            def mixing_weights():
                dve.wait_ge(mw_exp, 1)
                dve.tensor_scalar(mix[:, 2:4], mix[:, 0:2], 1.0, None, ALU.add).then_inc(mix_step, 1)
                dve.wait_ge(mix_step, 1)
                dve.reciprocal(mix[:, 4:6], mix[:, 2:4]).then_inc(mix_step, 1)
                dve.wait_ge(mix_step, 2)
                dve.tensor_copy(omw_16[:, :, :].rearrange("p a b -> p (a b)"), omw_col.broadcast_to([P, 16])
                                ).then_inc(mix_step, 1)

            dve.memset(k_op[ZROW:MAXROW, :, :], 0.0).then_inc(op_set, 1)
            ffn_moments(f1, 0, 0)
            ffn_moments(f1, 0, 1)
            dve.wait_ge(w_loaded, 16 * 3)
            dve.tensor_copy(w_f[:, :, :], w_int[:, :, :]).then_inc(w_cast, 1)

            def row_maxima(K, par, st, quarters=range(2 * GROUP)):
                for q in quarters:
                    n = 4 * st + q
                    dve.wait_ge(a_ready, at(32, K, n + 1))
                    dve.tensor_reduce(mx[:, par, q // 2, st, q % 2:q % 2 + 1], a_b[n % 3][:, :], AX.X, ALU.max
                                      ).then_inc(a_used, 1)

            def first_maxima(start, end):
                for n in range(start, end):
                    row_maxima(0, 0, n // 4, [n % 4])

            def phase1(pair, h):
                if isinstance(pair, int) and 2 * pair + h == 0:
                    mixing_weights()
                do(proj_thirds, pair, h, -2)
                do(lambda *c: ffn_hidden(f1, *c, 1), pair, h, 0)
                do(lambda *c: ffn_hidden(f1, *c, 2), pair, h, 0)
                do(memory_read, pair, h, -2)
                if isinstance(pair, int) and 2 * pair + h == CHUNKS - 1:
                    first_maxima(0, 3)
                if not (isinstance(pair, int) and pair < 0):
                    do(lambda *c: ffn_moments(f1, *c), pair, h, 2)
                do(lambda *c: ffn_hidden(f1, *c, 0), pair, h, 1)
                do(lambda *c: ffn_residual(f1, *c), pair, h, 0)
                do(proj_residues, pair, h, -1)
                do(proj_moments, pair, h, 0)

            def whole_maxima(K, par):
                dve.wait_ge(a_used, at(32, K, 32))
                dve.tensor_reduce(m16[:, par, :, :], mx[:, par, :, :, :], AX.X, ALU.max).then_inc(m_max, 1)

            def reciprocals(J, par):
                dve.wait_ge(o_sb, at(1, J, 1))
                dve.reciprocal(r_sum[:, par, :, :], o_s[:, par, :, :, DH]).then_inc(o_rec, 1)

            chunk_loop(dve, phase1)
            before, last = (CHUNKS // 2 - 1, 0), (CHUNKS // 2 - 1, 1)
            proj_thirds(*before)
            first_maxima(3, 6)
            memory_read(*before)
            first_maxima(6, 9)
            proj_residues(*last)
            first_maxima(9, 12)
            proj_thirds(*last)
            first_maxima(12, 15)
            memory_read(*last)
            first_maxima(15, 4 * TILES)
            whole_maxima(0, 0)
            for st in range(LEAD):
                row_maxima(1, 1, st)

            def pairs(it, first, last):
                for u in range(SLOTS):
                    J = it * SLOTS + u
                    for i in range(TILES):
                        n, st = ahead(i)
                        if not (last and u + n >= SLOTS):
                            row_maxima(J + n, (u + n) % 2, st)
                            if st == TILES - 1:
                                whole_maxima(J + n, (u + n) % 2)
                        if i == 3 and not (first and u == 0):
                            reciprocals(J - 1, (u - 1) % 2)
                        if last and i == 4 and u in AHEAD_CHUNK:
                            ffn_moments(f3, *AHEAD_CHUNK[u])
                        if last and u == 3 and i == 1:
                            ffn_hidden(f3, 0, 0, 0)

            attention_loop(dve, pairs)

            def phase3(pair, h):
                ffn_hidden(f3, pair, h, 1)
                if isinstance(pair, int) and 2 * pair + h == 0:
                    reciprocals(PAIRS - 1, 1)
                if not (isinstance(pair, int) and 2 * pair + h == 0):
                    do(lambda *c: ffn_moments(f3, *c), pair, h, 2)
                ffn_hidden(f3, pair, h, 2)
                do(lambda *c: ffn_hidden(f3, *c, 0), pair, h, 1)
                ffn_residual(f3, pair, h)

            phase3_loop(dve, phase3)

        @block.tensor
        def _(pe):
            mm = pe.matmul

            def ffn_transpose(f, pair, h, dst=tr_b):
                pe.wait_ge(f.xhat, at(2, pair, h + 1))
                if f is f1 and later(pair, h, 3):
                    pe.wait_ge(v_sb, at(2, pair, h - 2))
                for m in range(TPC):
                    i = pe.transpose(dst[:, P * m:P * m + P], x_hat[:, h, m, :], ident[:, :])
                i.then_inc(f.xt_ps, 1)

            def ffn_up(f, pair, h, k):
                n = KH * h + k
                if f is f1 and isinstance(pair, int) and 2 * pair + h + k == 0:
                    pe.wait_ge(w_cast, 1)
                if k == 0:
                    pe.wait_ge(f.xt, at(2, pair, h + 1))
                if later(pair, h, 1) or k == 2:
                    pe.wait_ge(f.hidden, at(2 * KH, pair, n - 1))
                mm(gate_b[n % 2][:, :], w_f[:, 0, P * k:P * k + P], x_t[:, h, :], start=True, stop=True)
                mm(up_b[n % 2][:, :], w_f[:, 1, P * k:P * k + P], x_t[:, h, :], start=True, stop=True).then_inc(f.gu, 1)

            def ffn_down(f, pair, h):
                if later(pair, h, 1):
                    pe.wait_ge(f.res, at(2, pair, h))
                for blocks in (range(KH - 1), range(KH - 1, KH)):
                    pe.wait_ge(f.hidden, at(2 * KH, pair, KH * h + blocks[-1] + 1))
                    for m in range(TPC):
                        for k in blocks:
                            i = mm(y_b[:, P * m:P * m + P], hid[:, h, k, P * m:P * m + P], w_f[:, 2, P * k:P * k + P],
                                   start=(m == 0 and k == 0), stop=(m == TPC - 1 and k == KH - 1))
                i.then_inc(f.y, 1)

            def proj_transpose(pair, h):
                pe.wait_ge(xn_ready, at(2, pair, h + 1))
                for m in range(TPC):
                    i = pe.transpose(tr_b[:, P * m:P * m + P], xn_hat[:, m, :], ident[:, :])
                i.then_inc(xn_ps, 1)

            def proj(pair, h):
                pe.wait_ge(xn_sb, at(2, pair, h + 1))
                if later(pair, h, 1):
                    pe.wait_ge(am_done, at(2, pair, h))
                mm(q_b[:, :], wq_s[:, :], xn_t[:, :], start=True, stop=True).then_inc(q_ps, 1)
                mm(k_b[0:KV, :], wk_s[:, :], xn_t[:, :], start=True, stop=True).then_inc(k_ps, 1)
                for m in range(TPC):
                    i = mm(tr_b[:, KV * m:KV * m + KV], xn_t[:, P * m:P * m + P], wv_s[:, :], start=True, stop=True)
                i.then_inc(v_ps, 1)

            def memory_product(pair, h):
                pe.wait_ge(q_elud, at(2, pair, h + 1))
                pe.wait_ge(q3_done, at(2, pair, h + 1))
                pe.wait_ge(k_res, at(2, pair, h + 1))
                for m in range(TPC):
                    mm(q_b[:, P * m:P * m + P], q_elu[:, P * m:P * m + P], mem_s[:, :], start=True, stop=True)
                    i = mm(k_b[:, GROUP * m:GROUP * (m + 1)], q_elu[:, P * m:P * m + P], norm_s[:, :],
                           start=True, stop=True)
                i.then_inc(am_ps, 1)

            pe.wait_ge(ident_set, 3)
            def stay_warm(n, out, eye=ident):
                for _ in range(n):
                    mm(out[:, 0:P], eye[:, :], eye[:, :], start=True, stop=True)

            stay_warm(14, misc_b)

            def max_scores(it, u, J, n, st, q):
                K, slot = J + n, (u + n) % SLOTS
                idx = 4 * st + q
                if idx == 0:
                    pe.wait_ge(loaded[slot], at(LOADS * 16, it + (u + n) // SLOTS, LOADS * 16))
                if not (isinstance(K, int) and K == 0 and idx < 3):
                    pe.wait_ge(a_used, at(32, K, (-1, 0, -2)[idx] if idx < 3 else idx - 2))
                g, half = q // 2, q % 2
                mm(a_b[idx % 3][:, :], q_op[0:MAXROW, slot, g, P * st:P * st + P],
                   k_op[0:MAXROW, slot, 512 * half:512 * half + 512], start=True, stop=True).then_inc(a_ready, 1)

            def first_scores(start, end):
                for n in range(start, end):
                    max_scores(0, 0, 0, n // (4 * TILES), n // 4 % TILES, n % 4)

            def phase1(pair, h):
                do(lambda *c: ffn_up(f1, *c, 1), pair, h, 0)
                do(lambda *c: ffn_up(f1, *c, 2), pair, h, 0)
                do(lambda *c: ffn_transpose(f1, *c), pair, h, 1)
                if isinstance(pair, int) and pair == 0 and h == 1:
                    pe.wait_ge(mem_loaded, 16 * 7)
                do(memory_product, pair, h, -2)
                do(lambda *c: ffn_up(f1, *c, 0), pair, h, 1)
                do(proj_transpose, pair, h, -1)
                if isinstance(pair, int) and 2 * pair + h == CHUNKS - 1:
                    pe.wait_ge(f1.hidden, KH * CHUNKS)
                    first_scores(0, 3)
                do(lambda *c: ffn_down(f1, *c), pair, h, 0)
                do(proj, pair, h, -1)

            def scores(J, u, i, q):
                idx = 4 * i + q
                if idx == 0:
                    pe.wait_ge(m_in, at(16, J, 16))
                if not (isinstance(J, int) and J == 0 and idx < 3):
                    pe.wait_ge(p_ready, at(32, J, (-1, 0, -2)[idx] if idx < 3 else idx - 2))
                g, half = q // 2, q % 2
                mm(t_b[idx % 3][:, :], k_op[0:MAXROW + PARTS, u, P * i:P * i + P],
                   q_op[0:MAXROW + PARTS, u, g, 512 * half:512 * half + 512], start=True, stop=True
                   ).then_inc(t_ready, 1)

            def weigh_values(J, par, i):
                pe.wait_ge(p_ready, at(32, J, 4 * i + 4))
                if i == 0:
                    pe.wait_ge(v9_ready, at(1, J, 1))
                    if not (isinstance(J, int) and J == 0):
                        pe.wait_ge(pv_sb, at(1, J, 0))
                for q in range(2 * GROUP):
                    m = mm(pv_b[VPAD * q:VPAD * q + VPAD, :], v9[:, par, i, :], probs[:, i % 2, q, :],
                           start=(i == 0), stop=(i == TILES - 1))
                if i == TILES - 1:
                    m.then_inc(pv_done, 1)

            def transpose_max(K, par):
                if not (isinstance(K, int) and K < 2):
                    pe.wait_ge(o_sb, at(1, K, -1))
                wait_alone(pe, m_split, at(5, K, 5))
                pe.transpose(misc_b[:, :].bitcast(bf16)[0:MCOLS, 0:P],
                             m_parts[:, par, :, :, :].rearrange("p a g t -> p (a g t)"), ident_b[:, :]
                             ).then_inc(m_ps, 1)

            def transpose_sums(J, par):
                pe.wait_ge(pv_sb, at(1, J, 1))
                if not (isinstance(J, int) and J == PAIRS - 1):
                    pe.wait_ge(m_sb, at(1, J, 2))
                else:
                    pe.wait_ge(o_sb, PAIRS - 1)
                for c in range(4):
                    i = pe.transpose(misc_b[:, P * c:P * c + P], o_t[:, par, P * c:P * c + P], ident[:, :])
                i.then_inc(o_ps, 1)

            chunk_loop(pe, phase1)
            before, last = (CHUNKS // 2 - 1, 0), (CHUNKS // 2 - 1, 1)
            first_scores(3, 6)
            stay_warm(8, banks[3])
            memory_product(*before)
            proj_transpose(*last)
            first_scores(6, 9)
            proj(*last)
            first_scores(9, 15)
            memory_product(*last)
            first_scores(15, 4 * (TILES + 1))
            for n in range(4 * (TILES + 1), 4 * (TILES + LEAD)):
                if n == 4 * (TILES + LEAD) - 5:
                    pe.wait_ge(am_done, CHUNKS)
                    pe.wait_ge(v_sb, CHUNKS)
                    transpose_max(0, 0)
                first_scores(n, n + 1)
                stay_warm(2, banks[3], ident_b)

            def pairs(it, first, last):
                for u in range(SLOTS):
                    J = it * SLOTS + u
                    for i in range(TILES):
                        n, st = ahead(i)
                        if i == 2 and not (first and u == 0):
                            transpose_sums(J - 1, (u - 1) % 2)
                        if i == 6 and not (last and u == SLOTS - 1):
                            transpose_max(J + 1, (u + 1) % 2)
                        for q in range(2 * GROUP):
                            scores(J, u, i, q)
                            if not (last and u + n >= SLOTS):
                                max_scores(it, u, J, n, st, q)
                        if i > 0:
                            weigh_values(J, u % 2, i - 1)
                        elif not (first and u == 0):
                            weigh_values(J - 1, (u - 1) % 2, TILES - 1)
                        if last and u == 2 and i == 5:
                            pe.wait_ge(a_used, 32 * PAIRS)
                            ffn_transpose(f3, 0, 0, banks[2])
                        if last and u == 2 and i == 6:
                            ffn_up(f3, 0, 0, 0)

            attention_loop(pe, pairs)
            weigh_values(PAIRS - 1, 1, TILES - 1)

            def phase3(pair, h):
                ffn_up(f3, pair, h, 1)
                if isinstance(pair, int) and 2 * pair + h == 0:
                    transpose_sums(PAIRS - 1, 1)
                do(lambda *c: ffn_transpose(f3, *c), pair, h, 1)
                ffn_up(f3, pair, h, 2)
                do(lambda *c: ffn_up(f3, *c, 0), pair, h, 1)
                ffn_down(f3, pair, h)

            phase3_loop(pe, phase3)


def kernel(L0_attn_x, L0_attn_Wq, L0_attn_Wk, L0_attn_Wv, L0_attn_memory, L0_attn_memory_norm,
           L0_attn_memory_weight, L0_ffn_w_gate, L0_ffn_w_up, L0_ffn_w_down):
    import numpy as np
    import concourse.bacc as bacc
    from concourse.bass_utils import run_bass_kernel_spmd

    arrays = {
        "x": L0_attn_x, "wq": L0_attn_Wq, "wk": L0_attn_Wk, "wv": L0_attn_Wv, "memory": L0_attn_memory,
        "memory_norm": L0_attn_memory_norm, "memory_weight": L0_attn_memory_weight,
        "wg_t": np.asarray(L0_ffn_w_gate).T, "wu_t": np.asarray(L0_ffn_w_up).T, "wd_t": np.asarray(L0_ffn_w_down).T,
    }
    arrays = {n: np.ascontiguousarray(a) for n, a in arrays.items()}
    nc = bacc.Bacc("TRN2", target_bir_lowering=False, num_devices=1)
    args = [nc.dram_tensor(n, a.shape, mybir.dt.from_np(a.dtype), kind="ExternalInput").ap()
            for n, a in arrays.items()]
    out = nc.dram_tensor("out", (B, S, D), mybir.dt.float32, kind="ExternalOutput").ap()
    build(nc, *args, out)
    run = run_bass_kernel_spmd(nc, [arrays], core_ids=[0])
    return run.results[0]["out"]
```
